# Optimizing a Trainium2 kernel written in Bass

```python
import numpy as np
import jax
import jax.numpy as jnp

def _softmax(x, axis=-1):
    return jax.nn.softmax(x, axis=axis)

def _gelu(x):
    return jax.nn.gelu(x, approximate=True)

def _silu(x):
    return jax.nn.silu(x)

def _sigmoid(x):
    return jax.nn.sigmoid(x)

def _layernorm(x, axis=-1, eps=1e-05):
    m = jnp.mean(x, axis=axis, keepdims=True)
    v = jnp.var(x, axis=axis, keepdims=True)
    return (x - m) / jnp.sqrt(v + eps)

def _scatter_add(tgt, idx, src, axis=0):
    return tgt.at[idx].add(src)

def _segment_sum(src, seg, n):
    return jax.ops.segment_sum(src, seg, n)
kernel_name = 'mk_early_fusion_d1_tok_img768_r4_7822e2'

def setup_inputs(seed: int=0):
    np.random.seed(seed)
    _w = jnp.asarray

    def _rec_inputs():
        import jax
        import jax.numpy as jnp
        _rk = jax.random.key(seed)
        x = -0.000356955 + 1 * jax.random.normal(jax.random.fold_in(_rk, 1), (32, 3, 224, 224), jnp.float32)
        txt = 0.00534838 + 0.580375 * jax.random.normal(jax.random.fold_in(_rk, 2), (32, 128, 192), jnp.float32)
        return (x, txt)
    x, txt = _rec_inputs()

    def _L0_tok_setup():
        import jax, jax.numpy as jnp
        import numpy as np
        C, H, W = (3, 224, 224)
        P = 14
        PS = H // P
        PATCH_DIM = C * PS * PS
        HIDDEN = 192

        def patchify(images):
            n = images.shape[0]
            x = images.reshape(n, C, P, PS, P, PS)
            x = x.transpose(0, 2, 4, 1, 3, 5)
            return x.reshape(n, P * P, PATCH_DIM)
        key = jax.random.key(seed)
        k1, k2, k3 = jax.random.split(key, 3)
        images = jax.random.normal(k1, (128, C, H, W), dtype=jnp.float32)
        bound = 1.0 / np.sqrt(PATCH_DIM)
        W_lin = jax.random.uniform(k2, (HIDDEN, PATCH_DIM), minval=-bound, maxval=bound, dtype=jnp.float32)
        b_lin = jax.random.uniform(k3, (HIDDEN,), minval=-bound, maxval=bound, dtype=jnp.float32)
        cls_token = jnp.ones((1, HIDDEN), dtype=jnp.float32)
        return {'images': images, 'W_lin': W_lin, 'b_lin': b_lin, 'cls_token': cls_token}
    _L0_tok_all = _L0_tok_setup()
    _L0_tok_in = {k: v for k, v in _L0_tok_all.items() if k in ('W_lin', 'b_lin', 'cls_token')}
    del _L0_tok_all

    def _L0_attn_setup():
        import jax, jax.numpy as jnp
        import numpy as np
        DIM, HEADS, SEQ_LEN = (192, 12, 1024)
        HEAD_DIM = DIM // HEADS
        RMS_EPS = 1.1920928955078125e-07
        ATTN_SCALE = 0.12

        def _rms_norm(x):
            return x * jax.lax.rsqrt(jnp.mean(x * x, axis=-1, keepdims=True) + RMS_EPS)

        def _rotary_tables(T, head_dim):
            freqs = (1.0 / 1024.0) ** jnp.linspace(0.0, 1.0, head_dim // 4, dtype=jnp.float32)
            freqs = jnp.concatenate([freqs, jnp.zeros(head_dim // 4, dtype=jnp.float32)])
            t = jnp.arange(T, dtype=jnp.float32)
            theta = t[:, None] * freqs[None, :]
            return (jnp.cos(theta), jnp.sin(theta))

        def _apply_rotary(x, cos, sin):
            x1, x2 = jnp.split(x.astype(jnp.float32), 2, axis=-1)
            c = cos[None, :, None, :]
            s = sin[None, :, None, :]
            y1 = x1 * c + x2 * s
            y2 = -x1 * s + x2 * c
            return jnp.concatenate([y1, y2], axis=-1).astype(x.dtype)
        key = jax.random.key(seed)
        k1, k2, k3 = jax.random.split(key, 3)
        x = jax.random.normal(k1, (1, SEQ_LEN, DIM), dtype=jnp.float32)
        std = 0.5 * DIM ** (-0.5)
        bound = 3.0 ** 0.5 * std
        qkv_w = jax.random.uniform(k2, (3, DIM, DIM), dtype=jnp.float32, minval=-bound, maxval=bound)
        c_proj_w = jax.random.normal(k3, (DIM, DIM), dtype=jnp.float32) * DIM ** (-0.5)
        return {'x': x, 'qkv_w': qkv_w, 'c_proj_w': c_proj_w}
    _L0_attn_all = _L0_attn_setup()
    _L0_attn_in = {k: v for k, v in _L0_attn_all.items() if k in ('qkv_w', 'c_proj_w')}
    del _L0_attn_all

    def _L0_ffn_setup():
        import jax, jax.numpy as jnp
        import numpy as np
        B, S, H, I = (4, 512, 192, 384)
        E, K = (3, 2)
        INIT = 0.02

        def _expert(x, gw, uw, dw):
            return jax.nn.silu(x @ gw) * (x @ uw) @ dw
        key = jax.random.key(seed)
        ks = jax.random.split(key, 8)
        f32 = jnp.float32
        return {'x': jax.random.normal(ks[0], (B, S, H), f32), 'shared_gate': jax.random.normal(ks[1], (H, I), f32) * INIT, 'shared_up': jax.random.normal(ks[2], (H, I), f32) * INIT, 'shared_down': jax.random.normal(ks[3], (I, H), f32) * INIT, 'routed_gate': jax.random.normal(ks[4], (E, H, I), f32) * INIT, 'routed_up': jax.random.normal(ks[5], (E, H, I), f32) * INIT, 'routed_down': jax.random.normal(ks[6], (E, I, H), f32) * INIT, 'router_w': jax.random.normal(ks[7], (H, E), f32) * INIT, 'routing_bias': jnp.zeros((E,), f32)}
    _L0_ffn_all = _L0_ffn_setup()
    _L0_ffn_in = {k: v for k, v in _L0_ffn_all.items() if k in ('shared_gate', 'shared_up', 'shared_down', 'routed_gate', 'routed_up', 'routed_down', 'router_w', 'routing_bias')}
    del _L0_ffn_all
    return {'x': x, 'txt': txt, 'L0_tok_W_lin': _L0_tok_in['W_lin'], 'L0_tok_b_lin': _L0_tok_in['b_lin'], 'L0_tok_cls_token': _L0_tok_in['cls_token'], 'L0_attn_qkv_w': _L0_attn_in['qkv_w'], 'L0_attn_c_proj_w': _L0_attn_in['c_proj_w'], 'L0_ffn_shared_gate': _L0_ffn_in['shared_gate'], 'L0_ffn_shared_up': _L0_ffn_in['shared_up'], 'L0_ffn_shared_down': _L0_ffn_in['shared_down'], 'L0_ffn_routed_gate': _L0_ffn_in['routed_gate'], 'L0_ffn_routed_up': _L0_ffn_in['routed_up'], 'L0_ffn_routed_down': _L0_ffn_in['routed_down'], 'L0_ffn_router_w': _L0_ffn_in['router_w'], 'L0_ffn_routing_bias': _L0_ffn_in['routing_bias']}

def reference(x, txt, L0_tok_W_lin, L0_tok_b_lin, L0_tok_cls_token, L0_attn_qkv_w, L0_attn_c_proj_w, L0_ffn_shared_gate, L0_ffn_shared_up, L0_ffn_shared_down, L0_ffn_routed_gate, L0_ffn_routed_up, L0_ffn_routed_down, L0_ffn_router_w, L0_ffn_routing_bias):
    import jax
    import jax.numpy as jnp

    def _L0_tok_ref(images, W_lin, b_lin, cls_token):
        import jax, jax.numpy as jnp
        import numpy as np
        C, H, W = (3, 224, 224)
        P = 14
        PS = H // P
        PATCH_DIM = C * PS * PS
        HIDDEN = 192

        def patchify(images):
            n = images.shape[0]
            x = images.reshape(n, C, P, PS, P, PS)
            x = x.transpose(0, 2, 4, 1, 3, 5)
            return x.reshape(n, P * P, PATCH_DIM)
        patches = patchify(images)
        hidden = jnp.einsum('npd,hd->nph', patches, W_lin) + b_lin
        n = images.shape[0]
        cls = jnp.broadcast_to(cls_token[None], (n, 1, HIDDEN))
        return jnp.concatenate([cls, hidden], axis=1)

    def _L0_attn_ref(x, qkv_w, c_proj_w):
        import jax, jax.numpy as jnp
        import numpy as np
        DIM, HEADS, SEQ_LEN = (192, 12, 1024)
        HEAD_DIM = DIM // HEADS
        RMS_EPS = 1.1920928955078125e-07
        ATTN_SCALE = 0.12

        def _rms_norm(x):
            return x * jax.lax.rsqrt(jnp.mean(x * x, axis=-1, keepdims=True) + RMS_EPS)

        def _rotary_tables(T, head_dim):
            freqs = (1.0 / 1024.0) ** jnp.linspace(0.0, 1.0, head_dim // 4, dtype=jnp.float32)
            freqs = jnp.concatenate([freqs, jnp.zeros(head_dim // 4, dtype=jnp.float32)])
            t = jnp.arange(T, dtype=jnp.float32)
            theta = t[:, None] * freqs[None, :]
            return (jnp.cos(theta), jnp.sin(theta))

        def _apply_rotary(x, cos, sin):
            x1, x2 = jnp.split(x.astype(jnp.float32), 2, axis=-1)
            c = cos[None, :, None, :]
            s = sin[None, :, None, :]
            y1 = x1 * c + x2 * s
            y2 = -x1 * s + x2 * c
            return jnp.concatenate([y1, y2], axis=-1).astype(x.dtype)
        B, T, dim = x.shape
        H, D = (HEADS, HEAD_DIM)
        qkv = jnp.einsum('btd,kfd->btkf', x, qkv_w)
        qkv = qkv.reshape(B, T, 3, H, D)
        q, k, v = (qkv[:, :, 0], qkv[:, :, 1], qkv[:, :, 2])
        q, k = (_rms_norm(q), _rms_norm(k))
        cos, sin = _rotary_tables(T, D)
        q, k = (_apply_rotary(q, cos, sin), _apply_rotary(k, cos, sin))
        scores = jnp.einsum('bthd,bshd->bhts', q, k) * ATTN_SCALE
        causal = jnp.tril(jnp.ones((T, T), dtype=bool))
        scores = jnp.where(causal[None, None], scores, jnp.finfo(scores.dtype).min)
        probs = jax.nn.softmax(scores, axis=-1)
        y = jnp.einsum('bhts,bshd->bthd', probs, v).reshape(B, T, dim)
        return y @ c_proj_w.T

    def _L0_ffn_ref(x, shared_gate, shared_up, shared_down, routed_gate, routed_up, routed_down, router_w, routing_bias):
        import jax, jax.numpy as jnp
        import numpy as np
        B, S, H, I = (4, 512, 192, 384)
        E, K = (3, 2)
        INIT = 0.02

        def _expert(x, gw, uw, dw):
            return jax.nn.silu(x @ gw) * (x @ uw) @ dw
        shared_out = _expert(x, shared_gate, shared_up, shared_down)
        routing_probs = jax.nn.sigmoid(x @ router_w + routing_bias)
        scores, indices = jax.lax.top_k(routing_probs, K)
        scores = scores / scores.sum(axis=-1, keepdims=True)
        combine_w = (jax.nn.one_hot(indices, E, dtype=x.dtype) * scores[..., None]).sum(axis=-2)
        g = jnp.einsum('bsh,ehi->ebsi', x, routed_gate)
        u = jnp.einsum('bsh,ehi->ebsi', x, routed_up)
        h = jax.nn.silu(g) * u
        out_e = jnp.einsum('ebsi,eih->ebsh', h, routed_down)
        combined = jnp.einsum('ebsh,bse->bsh', out_e, combine_w)
        return shared_out + combined
    h = _L0_tok_ref(x, L0_tok_W_lin, L0_tok_b_lin, L0_tok_cls_token)
    h = jnp.concatenate([h, txt], axis=1)
    h = h + _L0_attn_ref(_layernorm(h, axis=-1), L0_attn_qkv_w, L0_attn_c_proj_w)
    h = h + _L0_ffn_ref(_layernorm(h, axis=-1), L0_ffn_shared_gate, L0_ffn_shared_up, L0_ffn_shared_down, L0_ffn_routed_gate, L0_ffn_routed_up, L0_ffn_routed_down, L0_ffn_router_w, L0_ffn_routing_bias)
    return h

_drawn_inputs = setup_inputs


def setup_inputs(seed=0):
    import zlib

    import numpy as np

    out = dict(_drawn_inputs(seed))
    spreads = {'L0_tok_cls_token': (1.0, 0.2), 'L0_ffn_routing_bias': (0.0, 0.8)}
    factors = {'L0_ffn_routed_gate': 3.064,
     'L0_ffn_routed_up': 3.041,
     'L0_ffn_routed_down': 3.049,
     'L0_ffn_router_w': 5.581}
    for name, (base, spread) in spreads.items():
        noise = np.random.default_rng([zlib.crc32(name.encode()), seed]).standard_normal(out[name].shape)
        drawn = base * np.exp(spread * noise) if base else spread * noise
        out[name] = jnp.asarray(drawn.astype(out[name].dtype))
    for name, factor in factors.items():
        out[name] = (out[name] * factor).astype(out[name].dtype)
    return out
```

```python
from contextlib import ExitStack

import concourse.bass as bass
from concourse import mybir

F32 = mybir.dt.float32
F32R = mybir.dt.float32r
I32 = mybir.dt.int32
ALU = mybir.AluOpType
ACT = mybir.ActivationFunctionType
AX_X = mybir.AxisListType.X

BATCH, CHANNELS, IMAGE = 32, 3, 224
GRID = 14
PATCH = IMAGE // GRID
PATCH_DIM = CHANNELS * PATCH * PATCH
PATCHES = GRID * GRID
TXT, DIM = 128, 192
HEADS, HEAD_DIM = 12, 16
EXPERTS, INNER = 3, 384
FFNS = EXPERTS + 1
TOKENS = 1 + PATCHES + TXT
LN_EPS, RMS_EPS, ATTN_SCALE = 1e-5, 1.1920928955078125e-07, 0.12
RSQRT_MAGIC = 0x5F3759DF

P = 128
KT = PATCH_DIM // P
TILES = 3
PATCHES0 = PATCHES - P
REAL0 = PATCHES0 + 1
COLS0 = REAL0 + 1
COLS = COLS0 + 2 * P
TILE_AT = [0, COLS0, COLS0 + P]
TILE_COLS = [COLS0, P, P]
QK = 2 * DIM
REST = DIM - P
WIDE = DIM + REST
PAIRS = HEADS // 2
GROUP = 4
GROUPS = HEADS // GROUP
SLOT = 32
P_COLS = COLS + 3 * P
W_QKV, W_PROJ, W_FFN = 0, 3 * DIM, 4 * DIM
W_ALL = W_FFN + FFNS * 2 * INNER
CHUNKS = INNER // P
UNITS = FFNS * CHUNKS

ORDER = [
    ("residual", 0),
    ("qk_transpose", 0), ("qk_transpose", 1), ("embed", 0), ("qk_transpose", 2), ("unit", 0),
    ("qk_transpose", 3), ("embed", 1), ("qk_transpose", 4), ("unit", 1), ("qk_transpose", 5),
    ("score", 0), ("norm1", 0), ("unit", 2), ("score", 1), ("down", 0), ("score", 2), ("unit", 3),
    ("down", 1), ("value", 0), ("score", 3), ("unit", 4), ("score", 4), ("value", 1), ("unit", 5),
    ("score", 5), ("down", 2), ("norm1_transpose", 0), ("unit", 6), ("down", 3), ("value", 2),
    ("unit", 7), ("y_rows", 0), ("unit", 8), ("y_columns", 0), ("project_qk", 0), ("down", 4),
    ("project_y", 0), ("norm2", 0), ("unit", 9), ("down", 5), ("rotate", 0), ("project_v", 0),
    ("unit", 10), ("rotate", 1), ("unit", 11), ("norm2_transpose", 0), ("rotate", 2), ("down", 6),
    ("down", 7), ("router", 0),
]


class Signal:

    def __init__(self, sem, per_batch):
        self.sem, self.per_batch = sem, per_batch

    def at(self, batch, count):
        return self.per_batch * batch + count


def later(batch):
    return not (isinstance(batch, int) and batch == 0)


def build(nc, xp, txt, w_tok, bias, cls, w_a, w_b, w_down, w_router, b_router, rot_cos, rot_sin,
          mask0, mask1, identity, out):
    with ExitStack() as ctx:
        def sb(name, shape, dt=F32):
            return ctx.enter_context(nc.sbuf_tensor(name, shape, dt))

        def signal(name, per_batch):
            return Signal(ctx.enter_context(nc.semaphore(name)), per_batch)

        ident = sb("ident", [P, P])
        bias_rows = sb("bias_rows", [P, DIM])
        router_rows = sb("router_rows", [P, EXPERTS, DIM])
        router_bias = sb("router_bias", [P, EXPERTS])
        cos_t = sb("cos_t", [P, TILES, HEAD_DIM])
        sin_t = sb("sin_t", [P, TILES, HEAD_DIM // 2])
        causal0 = sb("causal0", [REAL0, COLS0])
        causal1 = sb("causal1", [P, P])
        w_tok_s = sb("w_tok_s", [P, KT, DIM])
        wa_hi = sb("wa_hi", [P, W_ALL], F32R)
        wa_lo = sb("wa_lo", [P, W_ALL], F32R)
        wb = sb("wb", [P, W_ALL], F32R)
        w_down_s = sb("w_down_s", [P, UNITS, DIM])
        x_s = sb("x_s", [P, KT, PATCHES])
        h0 = sb("h0", [P, TILES, DIM])
        stats = sb("stats", [P, TILES, 6])
        mean_var = sb("mean_var", [P, TILES, 2])
        rstd = sb("rstd", [P, 4, TILES])
        x_n = sb("x_n", [P, TILES, WIDE])
        xt = sb("xt", [P, 4, COLS], F32R)
        squares = sb("squares", [P, TILES * 2 * HEADS, HEAD_DIM])
        rms = sb("rms", [P, 4, TILES * 2 * HEADS])
        rotated = sb("rotated", [P, TILES * 2 * HEADS, HEAD_DIM])
        crossed = sb("crossed", [P, TILES, 2 * HEADS, HEAD_DIM // 2])
        normed = [sb(f"{a}_normed", [P, TILES * HEADS, HEAD_DIM]) for a in "qk"]
        qk_split = [sb(f"{a}_split", [P, TILES * HEADS, 4, HEAD_DIM], F32R) for a in "qk"]
        v_ones = sb("v_ones", [P, TILES, HEADS, SLOT])
        residual = sb("residual", [P, TILES, DIM])
        qt = sb("qt", [P, PAIRS, COLS], F32R)
        kt = sb("kt", [P, PAIRS, COLS], F32R)
        probs = sb("probs", [P, 2 * GROUP, P_COLS])
        y_cols = sb("y_cols", [P, GROUPS, COLS])
        row_sum = sb("row_sum", [P, TILES, HEADS])
        y_rows = sb("y_rows", [P, TILES, WIDE])
        yt = sb("yt", [P, 4, COLS], F32R)
        h1 = sb("h1", [P, TILES, DIM])
        stats2 = sb("stats2", [P, TILES, 6])
        mean_var2 = sb("mean_var2", [P, TILES, 2])
        rstd2 = sb("rstd2", [P, 4, TILES])
        x_n2 = sb("x_n2", [P, TILES, WIDE])
        xt2 = sb("xt2", [P, 4, COLS], F32R)
        junk = sb("junk", [P, DIM])
        logit = sb("logit", [P, TILES, EXPERTS])
        route = sb("route", [P, 8, TILES, EXPERTS])
        tanh_g = sb("tanh_g", [P, COLS])
        gated = sb("gated", [P, COLS])
        ht = sb("ht", [P, 2, CHUNKS, COLS])
        o = sb("o", [P, TILES, DIM])

        ps = ctx.enter_context(nc.psum_tensor("ps", [P, 8, 512], F32))
        GATE, UP, DOWN = 5, 6, 7

        s_const = ctx.enter_context(nc.semaphore("constants_loaded"))
        RAW = 4
        s_raw = [ctx.enter_context(nc.semaphore(f"raw_weights_{j}_loaded")) for j in range(RAW)]
        s_down = ctx.enter_context(nc.semaphore("raw_down_loaded"))
        s_split = ctx.enter_context(nc.semaphore("weights_split"))
        s_clear = ctx.enter_context(nc.semaphore("buffers_cleared"))
        s_halve = ctx.enter_context(nc.semaphore("down_halved"))
        x_loaded = signal("x_loaded", 16)
        txt_loaded = signal("txt_loaded", 16)
        stored = signal("stored", 64)
        embedded = signal("embedded", 2)
        n1_turned = signal("n1_turned", 2)
        qk_done = signal("qk_done", 3)
        v_done = signal("v_done", 2)
        qk_turned = signal("qk_turned", 2 * PAIRS)
        score0_done = signal("score0_done", PAIRS)
        score1_done = signal("score1_done", PAIRS)
        value_done = signal("value_done", GROUPS)
        y_turned = signal("y_turned", TILES)
        yt_turned = signal("yt_turned", 2)
        proj_done = signal("proj_done", 2)
        n2_turned = signal("n2_turned", 2)
        gate_done = signal("gate_done", UNITS)
        up_done = signal("up_done", UNITS)
        down_done = signal("down_done", 2 * FFNS)
        res_kept = signal("res_kept", 1)
        n1_applied = signal("n1_applied", 1)
        xt_hi = signal("xt_hi", 2)
        squared = signal("squared", 1)
        qk_hi = signal("qk_hi", 2)
        v_kept = signal("v_kept", 2)
        qt_kept = signal("qt_kept", PAIRS)
        exp0_done = signal("exp0_done", PAIRS)
        exp1_done = signal("exp1_done", PAIRS)
        y_kept = signal("y_kept", GROUPS)
        yt_hi = signal("yt_hi", 2)
        n2_applied = signal("n2_applied", 1)
        xt2_hi = signal("xt2_hi", 2)
        tanh_done = signal("tanh_done", UNITS)
        exp_logit = signal("exp_logit", 1)
        h0_ready = signal("h0_ready", 2)
        n1_ready = signal("n1_ready", 1)
        xt_lo = signal("xt_lo", 2)
        rot_ready = signal("rot_ready", 2)
        qk_lo = signal("qk_lo", 2)
        kt_kept = signal("kt_kept", PAIRS)
        masked = signal("masked", PAIRS)
        y_ready = signal("y_ready", 1)
        yt_lo = signal("yt_lo", 2)
        h1_ready = signal("h1_ready", 1)
        n2_ready = signal("n2_ready", 1)
        xt2_lo = signal("xt2_lo", 2)
        logit_ready = signal("logit_ready", 1)
        gate_used = signal("gate_used", UNITS)
        h_ready = signal("h_ready", UNITS)
        summed = signal("summed", 2 * FFNS)
        chain1 = signal("chain1", 31)
        chain2 = signal("chain2", 32)

        def shaped(view, dims, offset=0):
            return bass.AP(view.tensor, view.offset + offset, [list(view.ap[0]), *dims])

        def f32(view):
            return view.bitcast(F32)

        def hi_lo(a, part):
            first, step = ((0, 2), (0, 3))[a] if part == 0 else ((1, 2), (1, 1))[a]
            return shaped(qk_split[a][:], [[4 * HEAD_DIM, TILES * HEADS], [step * HEAD_DIM, 2], [1, HEAD_DIM]],
                          first * HEAD_DIM)

        piece = W_ALL // RAW
        raw = probs[:, :, :].rearrange("p a b -> p (a b)")
        raw_a = [raw[:, (2 * (j % 2)) * piece:(2 * (j % 2) + 1) * piece] for j in range(RAW)]
        raw_b = [raw[:, (2 * (j % 2) + 1) * piece:(2 * (j % 2) + 2) * piece] for j in range(RAW)]

        block = ctx.enter_context(nc.Block())

        def turns(engine, turn):
            turn(-1, True, False, False)
            turn(0, True, True, False)
            turn(1, True, True, True)
            with engine.Fori(2, BATCH - 1) as i:
                turn(i, True, True, True)
            turn(BATCH - 1, False, True, True)
            turn(BATCH, False, False, True)

        @block.sync
        def _(sp):
            sp.dma_start(w_tok_s[:], w_tok).then_inc(s_const, 16)
            sp.dma_start(x_s[:], xp[0]).then_inc(x_loaded.sem, 16)
            sp.dma_start(bias_rows[:], bias.partition_broadcast(P)).then_inc(s_const, 16)
            sp.wait_ge(s_clear, 1)
            sp.dma_start(h0[REAL0 - 1:REAL0, 0, :], cls).then_inc(s_const, 16)
            sp.dma_start(h0[:, 2, :], txt[0]).then_inc(txt_loaded.sem, 16)
            sp.dma_start(ident[:], identity).then_inc(s_const, 16)
            sp.dma_start(cos_t[:], rot_cos).then_inc(s_const, 16)
            sp.dma_start(sin_t[:], rot_sin).then_inc(s_const, 16)
            sp.dma_start(causal0[:], mask0).then_inc(s_const, 16)
            sp.dma_start(causal1[:], mask1).then_inc(s_const, 16)
            sp.dma_start(router_rows[:].rearrange("p e d -> p (e d)"), w_router.partition_broadcast(P)).then_inc(s_const, 16)
            sp.dma_start(router_bias[:], b_router.partition_broadcast(P)).then_inc(s_const, 16)
            for j in range(RAW):
                if j >= 2:
                    sp.wait_ge(s_split, 4 * (j - 1))
                sp.dma_start(raw_a[j], w_a[:, j * piece:(j + 1) * piece]).then_inc(s_raw[j], 16)
                sp.dma_start(raw_b[j], w_b[:, j * piece:(j + 1) * piece]).then_inc(s_raw[j], 16)
            sp.dma_start(w_down_s[:], w_down).then_inc(s_down, 16)

            def turn(i, s1, s2, s3):
                b1, b2, b3 = i + 1, i, i - 1
                if s1 and s2:
                    sp.wait_ge(res_kept.sem, res_kept.at(b2, 1))
                    sp.wait_ge(n1_applied.sem, n1_applied.at(b2, 1))
                    sp.dma_start(h0[:, 2, :], txt[b1]).then_inc(txt_loaded.sem, 16)
                if s1 and not (isinstance(i, int) and b1 + 1 >= BATCH):
                    sp.wait_ge(embedded.sem, embedded.at(b1, 2))
                    sp.dma_start(x_s[:], xp[b1 + 1]).then_inc(x_loaded.sem, 16)
                if s3:
                    sp.wait_ge(summed.sem, summed.at(b3, 2 * FFNS))
                    sp.dma_start(out[b3, 1:REAL0, :], o[0:PATCHES0, 0, :]).then_inc(stored.sem, 16)
                    sp.dma_start(out[b3, 0:1, :], o[PATCHES0:REAL0, 0, :]).then_inc(stored.sem, 16)
                    sp.dma_start(out[b3, REAL0:REAL0 + P, :], o[:, 1, :]).then_inc(stored.sem, 16)
                    sp.dma_start(out[b3, REAL0 + P:TOKENS, :], o[:, 2, :]).then_inc(stored.sem, 16)

            turn(-1, True, False, False)
            turn(0, True, True, False)
            turn(1, True, True, True)
            with sp.Fori(2, BATCH - 2) as i:
                turn(i, True, True, True)
            turn(BATCH - 2, True, True, True)
            turn(BATCH - 1, False, True, True)
            turn(BATCH, False, False, True)
            sp.wait_ge(stored.sem, stored.at(BATCH - 1, 64))

        @block.tensor
        def _(pe):
            def mm(dst, lhs, rhs, first, last):
                return nc.tensor.matmul(dst, lhs, rhs, start=first, stop=last)

            def turned(dst, src):
                return nc.tensor.transpose(dst, src, ident[0:src.shape[0], 0:src.shape[0]])

            def tile_cols(t):
                return slice(TILE_AT[t], TILE_AT[t] + TILE_COLS[t])

            def row_cols(t):
                return slice(TILE_AT[t], TILE_AT[t] + P)

            def split_by_rows(dst, act_t, cols, w0, w1):
                w = slice(w0, w1)
                mm(dst, act_t[:, 0, cols], wa_hi[:, w], True, False)
                mm(dst, act_t[:, 0, cols], wa_lo[:, w], False, False)
                mm(dst, act_t[:, 1, cols], wa_hi[:, w], False, False)
                mm(dst, act_t[:, 2, cols], wb[:, w], False, False)
                return mm(dst, act_t[:, 3, cols], wb[:, w], False, True)

            def split_by_cols(dst, act_t, w0):
                w = slice(w0, w0 + P)
                mm(dst, wa_hi[:, w], act_t[:, 0, :], True, False)
                mm(dst, wa_hi[:, w], act_t[:, 1, :], False, False)
                mm(dst, wa_lo[:, w], act_t[:, 0, :], False, False)
                mm(dst, wb[:, w], act_t[:, 2, :], False, False)
                return mm(dst, wb[:, w], act_t[:, 3, :], False, True)

            def turn_rows(rows, bank_a, bank_b, done):
                for t in range(TILES):
                    last = turned(ps[:, bank_a, tile_cols(t)], rows[0:TILE_COLS[t], t, 0:P])
                last.then_inc(done.sem, 1)
                for t in range(TILES):
                    last = turned(ps[:, bank_b, tile_cols(t)], rows[0:TILE_COLS[t], t, P:WIDE])
                last.then_inc(done.sem, 1)

            def qk_transpose(m, b, s1):
                if m == 0:
                    pe.wait_ge(qk_hi.sem, qk_hi.at(b, 2))
                    pe.wait_ge(qk_lo.sem, qk_lo.at(b, 2))
                    if later(b):
                        pe.wait_ge(xt2_hi.sem, xt2_hi.at(b - 1, 2))
                    if later(b):
                        pe.wait_ge(xt2_lo.sem, xt2_lo.at(b - 1, 2))
                for n in (2 * m, 2 * m + 1):
                    bank = n % 4
                    if n >= 4:
                        kept = kt_kept if n % 2 else qt_kept
                        pe.wait_ge(kept.sem, kept.at(b, m - 1))
                    for t in range(TILES):
                        r = TILE_COLS[t]
                        heads = slice(t * HEADS + 2 * m, t * HEADS + 2 * m + 2)
                        v = f32(qk_split[n % 2][0:r, heads]).rearrange("p h s d -> p (h s d)")
                        last = turned(ps[:, bank, tile_cols(t)], v)
                    last.then_inc(qk_turned.sem, 1)

            def embed(t, b):
                if t == 0:
                    pe.wait_ge(x_loaded.sem, x_loaded.at(b, 16))
                n = [PATCHES0, P][t]
                at = [0, PATCHES0][t]
                for j in range(KT):
                    last = mm(ps[0:n, 4, t * DIM:(t + 1) * DIM], x_s[:, j, at:at + n], w_tok_s[:, j, :], j == 0, j == KT - 1)
                last.then_inc(embedded.sem, 1)

            def score(p, b):
                if p == 0:
                    pe.wait_ge(qt_kept.sem, qt_kept.at(b, PAIRS))
                    pe.wait_ge(kt_kept.sem, kt_kept.at(b, PAIRS))
                if p:
                    pe.wait_ge(exp0_done.sem, exp0_done.at(b, p))
                for j in range(2):
                    r = slice(64 * j, 64 * j + 64)
                    last = mm(ps[0:REAL0, j, 0:COLS], kt[r, p, 0:REAL0], qt[r, p, :], True, True)
                last.then_inc(score0_done.sem, 1)
                if p:
                    pe.wait_ge(exp1_done.sem, exp1_done.at(b, p))
                for j in range(2):
                    r = slice(64 * j, 64 * j + 64)
                    mm(ps[:, 2 + j, 0:2 * P], kt[r, p, tile_cols(1)], qt[r, p, TILE_AT[1]:COLS], True, True)
                    last = mm(ps[:, 2 + j, 2 * P:3 * P], kt[r, p, tile_cols(2)], qt[r, p, tile_cols(2)], True, True)
                last.then_inc(score1_done.sem, 1)

            def value(g, b, s1):
                if g == 0:
                    pe.wait_ge(v_kept.sem, v_kept.at(b, 2))
                    if s1:
                        pe.wait_ge(h0_ready.sem, h0_ready.at(b + 1, 2))
                else:
                    pe.wait_ge(y_kept.sem, y_kept.at(b, g))
                pe.wait_ge(masked.sem, masked.at(b, 2 * g + 2))
                base = GROUP * (g % 2)
                for t in range(TILES):
                    k = REAL0 if t == 0 else P
                    at = [0, COLS, COLS + 2 * P][t]
                    for j in range(GROUP):
                        last = mm(ps[SLOT * j:SLOT * j + SLOT, 4, TILE_AT[t]:COLS], v_ones[0:k, t, GROUP * g + j, :],
                                  probs[0:k, base + j, at:at + COLS - TILE_AT[t]], t == 0, t == TILES - 1)
                last.then_inc(value_done.sem, 1)

            def y_to_rows(b, s1):
                pe.wait_ge(y_kept.sem, y_kept.at(b, GROUPS))
                pe.wait_ge(exp0_done.sem, exp0_done.at(b, PAIRS))
                pe.wait_ge(exp1_done.sem, exp1_done.at(b, PAIRS))
                if s1:
                    pe.wait_ge(xt_hi.sem, xt_hi.at(b + 1, 2))
                    pe.wait_ge(xt_lo.sem, xt_lo.at(b + 1, 2))
                for t in range(TILES):
                    for g in range(GROUPS):
                        last = turned(ps[:, t, g * P:(g + 1) * P], y_cols[:, g, row_cols(t)])
                    last.then_inc(y_turned.sem, 1)

            def project_qk(b, s2):
                pe.wait_ge(xt_hi.sem, xt_hi.at(b, 2))
                pe.wait_ge(xt_lo.sem, xt_lo.at(b, 2))
                if s2:
                    if later(b):
                        pe.wait_ge(y_ready.sem, y_ready.at(b - 1, 1))
                for t in range(TILES):
                    split_by_rows(ps[:, t, 0:QK], xt, row_cols(t), W_QKV, W_QKV + QK).then_inc(qk_done.sem, 1)

            def project_v(b, s2):
                if s2:
                    if later(b):
                        pe.wait_ge(h1_ready.sem, h1_ready.at(b - 1, 1))
                for t in range(TILES):
                    last = split_by_rows(ps[:, 3 + t // 2, (t % 2) * DIM:(t % 2 + 1) * DIM], xt, row_cols(t),
                                         W_QKV + QK, W_QKV + 3 * DIM)
                    if t:
                        last.then_inc(v_done.sem, 1)

            def project_y(b):
                pe.wait_ge(yt_hi.sem, yt_hi.at(b, 2))
                pe.wait_ge(yt_lo.sem, yt_lo.at(b, 2))
                for t in range(TILES):
                    last = split_by_rows(ps[:, 3 + t // 2, (t % 2) * DIM:(t % 2 + 1) * DIM], yt, row_cols(t),
                                         W_PROJ, W_PROJ + DIM)
                    if t:
                        last.then_inc(proj_done.sem, 1)

            def unit(k, b):
                w = W_FFN + (k // CHUNKS) * 2 * INNER + (k % CHUNKS) * P
                if k == 0:
                    pe.wait_ge(xt2_hi.sem, xt2_hi.at(b, 2))
                    pe.wait_ge(xt2_lo.sem, xt2_lo.at(b, 2))
                if k or later(b):
                    pe.wait_ge(gate_used.sem, gate_used.at(b, k))
                split_by_cols(ps[:, GATE, 0:COLS], xt2, w).then_inc(gate_done.sem, 1)
                if k or later(b):
                    pe.wait_ge(h_ready.sem, h_ready.at(b, k))
                split_by_cols(ps[:, UP, 0:COLS], xt2, w + INNER).then_inc(up_done.sem, 1)

            def down(n, b):
                e = n // 2
                if n % 2 == 0:
                    pe.wait_ge(h_ready.sem, h_ready.at(b, CHUNKS * (e + 1)))
                if n or later(b):
                    pe.wait_ge(summed.sem, summed.at(b, n))
                for t in ([0, 1] if n % 2 == 0 else [2]):
                    for c in range(CHUNKS):
                        last = mm(ps[:, DOWN, (t % 2) * DIM:(t % 2 + 1) * DIM], ht[:, e % 2, c, row_cols(t)],
                                  w_down_s[:, CHUNKS * e + c, :], c == 0, c == CHUNKS - 1)
                last.then_inc(down_done.sem, 1)

            def turn(i, s1, s2, s3):
                b1, b2, b3 = i + 1, i, i - 1
                for step, k in ORDER:
                    if step == "qk_transpose" and s2:
                        qk_transpose(k, b2, s1)
                    if step == "embed" and s1:
                        embed(k, b1)
                    if step == "score" and s2:
                        score(k, b2)
                    if step == "value" and s2:
                        value(k, b2, s1)
                    if step == "norm1_transpose" and s1:
                        pe.wait_ge(n1_applied.sem, n1_applied.at(b1, 1))
                        if s2:
                            pe.wait_ge(exp0_done.sem, exp0_done.at(b2, PAIRS))
                        turn_rows(x_n, 0, 1, n1_turned)
                    if step == "y_rows" and s2:
                        y_to_rows(b2, s1)
                    if step == "y_columns" and s2:
                        pe.wait_ge(y_ready.sem, y_ready.at(b2, 1))
                        turn_rows(y_rows, 3, 4, yt_turned)
                    if step == "project_y" and s2:
                        project_y(b2)
                    if step == "project_qk" and s1:
                        project_qk(b1, s2)
                    if step == "project_v" and s1:
                        project_v(b1, s2)
                    if step == "norm2_transpose" and s2:
                        pe.wait_ge(n2_applied.sem, n2_applied.at(b2, 1))
                        if s1:
                            pe.wait_ge(v_kept.sem, v_kept.at(b1, 2))
                        turn_rows(x_n2, 3, 4, n2_turned)
                    if step == "unit" and s3:
                        unit(k, b3)
                    if step == "down" and s3:
                        down(k, b3)

            pe.wait_ge(s_const, 16 * 10)
            pe.wait_ge(s_split, 4 * RAW)
            pe.wait_ge(s_halve, 1)
            turns(pe, turn)

        @block.scalar
        def _(act):
            def copy(dst, src):
                return nc.scalar.activation(dst, src, ACT.Copy)

            def apply_norm(dst, src, coef):
                for t in range(TILES):
                    for a, z in ((0, 0), (P, REST)):
                        last = nc.scalar.activation(dst[:, t, a + z:DIM + z], src[:, t, a:DIM], ACT.Identity,
                                                    bias=coef[:, 3, t:t + 1], scale=coef[:, 0, t:t + 1])
                return last

            def turn(i, s1, s2, s3):
                b1, b2, b3 = i + 1, i, i - 1
                for step, k in ORDER:
                    if step == "residual" and s2:
                        act.wait_ge(h0_ready.sem, h0_ready.at(b2, 2))
                        act.wait_ge(txt_loaded.sem, txt_loaded.at(b2, 16))
                        if later(b2):
                            act.wait_ge(h1_ready.sem, h1_ready.at(b2 - 1, 1))
                        copy(residual[:], h0[:]).then_inc(res_kept.sem, 1)
                    if step == "norm1" and s1:
                        act.wait_ge(n1_ready.sem, n1_ready.at(b1, 1))
                        if later(b1):
                            act.wait_ge(n1_turned.sem, n1_turned.at(b1 - 1, 2))
                        apply_norm(x_n, h0, rstd).then_inc(n1_applied.sem, 1)
                    if step == "norm1_transpose" and s1:
                        if later(b1):
                            act.wait_ge(v_done.sem, v_done.at(b1 - 1, 2))
                        for h in range(2):
                            act.wait_ge(n1_turned.sem, n1_turned.at(b1, h + 1))
                            copy(xt[:, 2 * h, :], ps[:, h, 0:COLS]).then_inc(xt_hi.sem, 1)
                    if step == "project_qk" and s1:
                        act.wait_ge(qk_done.sem, qk_done.at(b1, TILES))
                        sq = squares[:].rearrange("p (t h) d -> p t (h d)", t=TILES)
                        nc.scalar.activation(sq, ps[:, 0:TILES, 0:QK], ACT.Square,
                                             scale=HEAD_DIM ** -0.5).then_inc(squared.sem, 1)
                    if step == "project_v" and s1:
                        if later(b1):
                            act.wait_ge(value_done.sem, value_done.at(b1 - 1, GROUPS))
                        for h, n in enumerate((2, 1)):
                            act.wait_ge(v_done.sem, v_done.at(b1, h + 1))
                            copy(v_ones[:, 2 * h:2 * h + n, :, 0:HEAD_DIM],
                                 ps[:, 3 + h, 0:n * DIM].rearrange("p (t h d) -> p t h d", t=n, h=HEADS)).then_inc(v_kept.sem, 1)
                    if step == "rotate" and k == 2 and s1:
                        act.wait_ge(rot_ready.sem, rot_ready.at(b1, 2))
                        if later(b1):
                            act.wait_ge(qk_turned.sem, qk_turned.at(b1 - 1, 2 * PAIRS))
                        for a in range(2):
                            x = shaped(normed[a][:], [[HEAD_DIM, TILES * HEADS], [0, 2], [1, HEAD_DIM]])
                            copy(hi_lo(a, 0), x).then_inc(qk_hi.sem, 1)
                    if step == "qk_transpose" and s2:
                        if k == 0:
                            if later(b2):
                                act.wait_ge(score1_done.sem, score1_done.at(b2 - 1, PAIRS))
                        act.wait_ge(qk_turned.sem, qk_turned.at(b2, 2 * k + 1))
                        copy(qt[:, k, :], ps[:, (2 * k) % 4, 0:COLS]).then_inc(qt_kept.sem, 1)
                    if step == "score" and s2:
                        slot = (2 * k) % (2 * GROUP)
                        if k == 0:
                            if later(b2):
                                act.wait_ge(value_done.sem, value_done.at(b2 - 1, GROUPS))
                        if k == 4:
                            act.wait_ge(value_done.sem, value_done.at(b2, 1))
                        act.wait_ge(score0_done.sem, score0_done.at(b2, k + 1))
                        nc.scalar.activation(probs[0:REAL0, slot:slot + 2, 0:COLS], ps[0:REAL0, 0:2, 0:COLS],
                                             ACT.Exp, scale=ATTN_SCALE).then_inc(exp0_done.sem, 1)
                        act.wait_ge(score1_done.sem, score1_done.at(b2, k + 1))
                        nc.scalar.activation(probs[:, slot:slot + 2, COLS:P_COLS], ps[:, 2:4, 0:3 * P],
                                             ACT.Exp, scale=ATTN_SCALE).then_inc(exp1_done.sem, 1)
                    if step == "value" and s2:
                        if k == 0:
                            if later(b2):
                                act.wait_ge(y_turned.sem, y_turned.at(b2 - 1, TILES))
                        act.wait_ge(value_done.sem, value_done.at(b2, k + 1))
                        copy(y_cols[:, k, :], ps[:, 4, 0:COLS]).then_inc(y_kept.sem, 1)
                    if step == "y_columns" and s2:
                        if later(b2):
                            act.wait_ge(proj_done.sem, proj_done.at(b2 - 1, 2))
                        for h in range(2):
                            act.wait_ge(yt_turned.sem, yt_turned.at(b2, h + 1))
                            copy(yt[:, 2 * h, :], ps[:, 3 + h, 0:COLS]).then_inc(yt_hi.sem, 1)
                    if step == "norm2" and s2:
                        act.wait_ge(n2_ready.sem, n2_ready.at(b2, 1))
                        if later(b2):
                            act.wait_ge(n2_turned.sem, n2_turned.at(b2 - 1, 2))
                        apply_norm(x_n2, h1, rstd2).then_inc(n2_applied.sem, 1)
                    if step == "norm2_transpose" and s2:
                        if s3:
                            act.wait_ge(up_done.sem, up_done.at(b3, UNITS))
                        for h in range(2):
                            act.wait_ge(n2_turned.sem, n2_turned.at(b2, h + 1))
                            copy(xt2[:, 2 * h, :], ps[:, 3 + h, 0:COLS]).then_inc(xt2_hi.sem, 1)
                    if step == "router" and s2:
                        act.wait_ge(logit_ready.sem, logit_ready.at(b2, 1))
                        nc.scalar.activation(route[:, 0], logit[:], ACT.Exp, scale=-1.0).then_inc(exp_logit.sem, 1)
                    if step == "unit" and s3:
                        act.wait_ge(gate_done.sem, gate_done.at(b3, k + 1))
                        if k or later(b3):
                            act.wait_ge(gate_used.sem, gate_used.at(b3, k))
                        nc.scalar.activation(tanh_g[:], ps[:, GATE, 0:COLS], ACT.Tanh, scale=0.5).then_inc(tanh_done.sem, 1)

            turns(act, turn)

        @block.vector
        def _(dve):
            v = nc.vector
            steps = {chain1: 0, chain2: 0}

            def link(chain, b, instruction):
                instruction.then_inc(chain.sem, 1)
                steps[chain] += 1
                dve.wait_ge(chain.sem, chain.at(b, steps[chain]))

            def rsqrt(chain, b, x, y, tmp):
                link(chain, b, v.tensor_scalar(y.bitcast(I32), x.bitcast(I32), 1, None, ALU.logical_shift_right))
                link(chain, b, v.tensor_scalar(y.bitcast(I32), y.bitcast(I32), -1.0, float(RSQRT_MAGIC), ALU.mult, ALU.add))
                for _ in range(3):
                    link(chain, b, v.tensor_tensor(tmp, y, y, ALU.mult))
                    link(chain, b, v.scalar_tensor_tensor(out=tmp, in0=tmp, scalar=-0.5, in1=x, op0=ALU.mult, op1=ALU.mult))
                    link(chain, b, v.scalar_tensor_tensor(out=y, in0=tmp, scalar=1.5, in1=y, op0=ALU.add, op1=ALU.mult))

            def norm_stats(chain, b, rows, st, mv, coef, ready):
                for t in range(TILES):
                    last = v.bn_stats(st[:, t, :], rows[:, t, :])
                link(chain, b, last)
                v.tensor_copy(coef[:, 2, 0:1], st[:, 0, 0:1])
                for t in range(TILES):
                    last = v.bn_aggr(mv[:, t, :], st[:, t, :])
                link(chain, b, last)
                link(chain, b, v.tensor_scalar(coef[:, 1, :], mv[:, :, 1], LN_EPS, None, ALU.add))
                rsqrt(chain, b, coef[:, 1, :], coef[:, 0, :], coef[:, 2, :])
                v.scalar_tensor_tensor(out=coef[:, 3, :], in0=mv[:, :, 0], scalar=-1.0, in1=coef[:, 0, :],
                                       op0=ALU.mult, op1=ALU.mult).then_inc(ready.sem, 1)

            def keep_low(dst, src_bank, hi, hi_signal, b, lo_signal):
                for h in range(2):
                    dve.wait_ge(hi_signal.sem, hi_signal.at(b, h + 1))
                    v.tensor_tensor(dst[:, 2 * h + 1, :], ps[:, src_bank + h, 0:COLS], f32(dst[:, 2 * h, :]),
                                    ALU.subtract).then_inc(lo_signal.sem, 1)

            def rotate(part, b, s2):
                bank = ps[:, 0:TILES, 0:QK].rearrange("p t (h d) -> p t h d", h=2 * HEADS)
                rot = rotated[:].rearrange("p (t h) d -> p t h d", t=TILES)
                quarter, half = HEAD_DIM // 4, HEAD_DIM // 2
                if part == 0:
                    dve.wait_ge(squared.sem, squared.at(b, 1))
                    link(chain1, b, v.tensor_reduce(rms[:, 1, :], squares[:], AX_X, ALU.add))
                    link(chain1, b, v.tensor_scalar(rms[:, 1, :], rms[:, 1, :], RMS_EPS, None, ALU.add))
                    rsqrt(chain1, b, rms[:, 1, :], rms[:, 0, :], rms[:, 2, :])
                if part == 1:
                    c = shaped(cos_t[:], [[HEAD_DIM, TILES], [0, 2 * HEADS], [1, HEAD_DIM]])
                    v.tensor_tensor(rot, bank, c, ALU.mult)
                    for a in range(2):
                        s = shaped(sin_t[:, :, a * quarter:(a + 1) * quarter], [[half, TILES], [0, 2 * HEADS], [1, quarter]])
                        last = v.tensor_tensor(crossed[:, :, :, a * quarter:(a + 1) * quarter],
                                               bank[:, :, :, half * (1 - a):half * (1 - a) + quarter], s, ALU.mult)
                    link(chain1, b, last)
                    r = shaped(rotated[:], [[HEAD_DIM, TILES * 2 * HEADS], [half, 2], [1, quarter]])
                    cr = crossed[:].rearrange("p t h (a d) -> p (t h) a d", a=2)
                    link(chain1, b, v.tensor_tensor(r, r, cr, ALU.add))
                    if later(b):
                        dve.wait_ge(qk_hi.sem, qk_hi.at(b - 1, 2))
                    for a in range(2):
                        x = shaped(rotated[:], [[QK, TILES], [HEAD_DIM, HEADS], [1, HEAD_DIM]], a * DIM)
                        scale = shaped(rms[:, 0, :], [[2 * HEADS, TILES], [1, HEADS], [0, HEAD_DIM]], a * HEADS)
                        y = normed[a][:].rearrange("p (t h) d -> p t h d", t=TILES)
                        v.tensor_tensor(y, x, scale, ALU.mult).then_inc(rot_ready.sem, 1)
                if part == 2:
                    if later(b):
                        dve.wait_ge(qk_turned.sem, qk_turned.at(b - 1, 2 * PAIRS))
                    for a in range(2):
                        dve.wait_ge(qk_hi.sem, qk_hi.at(b, a + 1))
                        hi, lo = f32(hi_lo(a, 0)), hi_lo(a, 1)
                        link(chain1, b, v.tensor_tensor(lo[:, :, 0], normed[a][:], hi[:, :, 0], ALU.subtract))
                        v.tensor_copy(lo[:, :, 1], f32(lo[:, :, 0])).then_inc(qk_lo.sem, 1)

            def mask(p, b):
                slot = (2 * p) % (2 * GROUP)
                dve.wait_ge(exp0_done.sem, exp0_done.at(b, p + 1))
                d0 = probs[0:REAL0, slot:slot + 2, 0:COLS0]
                v.tensor_tensor(d0, d0, shaped(causal0[:], [[0, 2], [1, COLS0]]), ALU.mult)
                dve.wait_ge(exp1_done.sem, exp1_done.at(b, p + 1))
                d1 = probs[:, slot:slot + 2, COLS:P_COLS]
                d1 = shaped(d1, [[P_COLS, 2], [2 * P, 2], [1, P]])
                v.tensor_tensor(d1, d1, shaped(causal1[:], [[0, 2], [0, 2], [1, P]]), ALU.mult).then_inc(masked.sem, 1)

            def router(b):
                dve.wait_ge(n2_applied.sem, n2_applied.at(b, 1))
                for t in range(TILES):
                    for e in range(EXPERTS):
                        link(chain2, b, v.tensor_tensor_reduce(junk[:], x_n2[:, t, 0:DIM], router_rows[:, e, :], 1.0, 0.0,
                                                               ALU.mult, ALU.add, route[:, 1, t, e:e + 1]))
                bias3 = shaped(router_bias[:], [[0, TILES], [1, EXPERTS]])
                v.tensor_tensor(logit[:], route[:, 1], bias3, ALU.add).then_inc(logit_ready.sem, 1)
                dve.wait_ge(exp_logit.sem, exp_logit.at(b, 1))
                link(chain2, b, v.tensor_scalar(route[:, 1], route[:, 0], 1.0, None, ALU.add))
                link(chain2, b, v.reciprocal(route[:, 2], route[:, 1]))
                s = [route[:, 2, :, e] for e in range(EXPERTS)]
                keep = [route[:, 3, :, e] for e in range(EXPERTS)]
                m = [route[:, 4, :, e] for e in range(EXPERTS)]
                v.tensor_tensor(m[0], s[1], s[2], ALU.min)
                v.tensor_tensor(m[1], s[1], s[0], ALU.is_gt)
                v.tensor_tensor(m[2], s[0], s[1], ALU.min)
                link(chain2, b, v.tensor_tensor(keep[1], s[1], s[2], ALU.is_ge))
                v.tensor_tensor(keep[0], s[0], m[0], ALU.is_ge)
                v.tensor_tensor(keep[1], keep[1], m[1], ALU.max)
                link(chain2, b, v.tensor_tensor(keep[2], s[2], m[2], ALU.is_gt))
                link(chain2, b, v.tensor_tensor(route[:, 5], route[:, 2], route[:, 3], ALU.mult))
                link(chain2, b, v.tensor_reduce(route[:, 4, :, 0], route[:, 5], AX_X, ALU.add))
                link(chain2, b, v.reciprocal(route[:, 4, :, 1], route[:, 4, :, 0]))
                total = shaped(route[:, 4, :, 1:2], [[EXPERTS, TILES], [0, EXPERTS]])
                link(chain2, b, v.tensor_tensor(route[:, 6], route[:, 5], total, ALU.mult))

            def unit(k, b):
                if k or later(b):
                    dve.wait_ge(h_ready.sem, h_ready.at(b, k))
                dve.wait_ge(tanh_done.sem, tanh_done.at(b, k + 1))
                v.scalar_tensor_tensor(out=gated[:], in0=tanh_g[:], scalar=1.0, in1=ps[:, GATE, 0:COLS],
                                       op0=ALU.add, op1=ALU.mult).then_inc(gate_used.sem, 1)
                dve.wait_ge(up_done.sem, up_done.at(b, k + 1))
                dve.wait_ge(gate_used.sem, gate_used.at(b, k + 1))
                v.tensor_tensor(ht[:, (k // CHUNKS) % 2, k % CHUNKS, :], gated[:], ps[:, UP, 0:COLS],
                                ALU.mult).then_inc(h_ready.sem, 1)

            def down(n, b):
                e = n // 2
                dve.wait_ge(down_done.sem, down_done.at(b, n + 1))
                if n == 0:
                    if later(b):
                        dve.wait_ge(stored.sem, stored.at(b - 1, 64))
                tiles = [0, 1] if n % 2 == 0 else [2]
                if e:
                    dve.wait_ge(summed.sem, summed.at(b, n - 1))
                for t in tiles:
                    d = ps[:, DOWN, (t % 2) * DIM:(t % 2 + 1) * DIM]
                    if e == 0:
                        last = v.tensor_tensor(o[:, t, :], d, h1[:, t, :], ALU.add)
                    else:
                        last = v.scalar_tensor_tensor(out=o[:, t, :], in0=d, scalar=route[:, 6, t, e - 1:e],
                                                      in1=o[:, t, :], op0=ALU.mult, op1=ALU.add)
                last.then_inc(summed.sem, 1)

            def turn(i, s1, s2, s3):
                b1, b2, b3 = i + 1, i, i - 1
                steps[chain1] = steps[chain2] = 0
                for step, k in ORDER:
                    if step == "qk_transpose" and s2:
                        if k == 0:
                            if later(b2):
                                dve.wait_ge(score1_done.sem, score1_done.at(b2 - 1, PAIRS))
                        dve.wait_ge(qk_turned.sem, qk_turned.at(b2, 2 * k + 2))
                        v.tensor_copy(kt[:, k, :], ps[:, (2 * k + 1) % 4, 0:COLS]).then_inc(kt_kept.sem, 1)
                    if step == "embed" and k == 1 and s1:
                        dve.wait_ge(embedded.sem, embedded.at(b1, 2))
                        if s2:
                            dve.wait_ge(res_kept.sem, res_kept.at(b2, 1))
                        for t, n in enumerate((PATCHES0, P)):
                            v.tensor_tensor(h0[0:n, t, :], ps[0:n, 4, t * DIM:(t + 1) * DIM], bias_rows[0:n, :],
                                            ALU.add).then_inc(h0_ready.sem, 1)
                    if step == "norm1" and s1:
                        dve.wait_ge(txt_loaded.sem, txt_loaded.at(b1, 16))
                        dve.wait_ge(h0_ready.sem, h0_ready.at(b1, 2))
                        if later(b1):
                            dve.wait_ge(n1_applied.sem, n1_applied.at(b1 - 1, 1))
                        norm_stats(chain1, b1, h0, stats, mean_var, rstd, n1_ready)
                    if step == "norm1_transpose" and s1:
                        keep_low(xt, 0, None, xt_hi, b1, xt_lo)
                    if step == "rotate" and s1:
                        rotate(k, b1, s2)
                    if step == "score" and s2:
                        mask(k, b2)
                    if step == "y_rows" and s2:
                        dve.wait_ge(y_turned.sem, y_turned.at(b2, TILES))
                        yr = ps[:, 0:TILES, 0:QK].rearrange("p t (h s) -> p t h s", h=HEADS)
                        link(chain2, b2, v.reciprocal(row_sum[:], yr[:, :, :, HEAD_DIM]))
                        if later(b2):
                            dve.wait_ge(yt_turned.sem, yt_turned.at(b2 - 1, 2))
                        for at, first in ((0, 0), (DIM, P // HEAD_DIM)):
                            n = HEADS - first
                            last = v.tensor_tensor(shaped(y_rows[:], [[WIDE, TILES], [HEAD_DIM, n], [1, HEAD_DIM]], at),
                                                   yr[:, :, first:HEADS, 0:HEAD_DIM],
                                                   shaped(row_sum[:], [[HEADS, TILES], [1, n], [0, HEAD_DIM]], first),
                                                   ALU.mult)
                        last.then_inc(y_ready.sem, 1)
                    if step == "y_columns" and s2:
                        keep_low(yt, 3, None, yt_hi, b2, yt_lo)
                    if step == "project_y" and s2:
                        for h, n in enumerate((2, 1)):
                            dve.wait_ge(proj_done.sem, proj_done.at(b2, h + 1))
                            dve.wait_ge(res_kept.sem, res_kept.at(b2, 1))
                            last = v.tensor_tensor(h1[:, 2 * h:2 * h + n, :],
                                                   ps[:, 3 + h, 0:n * DIM].rearrange("p (t d) -> p t d", t=n),
                                                   residual[:, 2 * h:2 * h + n, :], ALU.add)
                        last.then_inc(h1_ready.sem, 1)
                    if step == "norm2" and s2:
                        dve.wait_ge(h1_ready.sem, h1_ready.at(b2, 1))
                        if later(b2):
                            dve.wait_ge(n2_applied.sem, n2_applied.at(b2 - 1, 1))
                        norm_stats(chain2, b2, h1, stats2, mean_var2, rstd2, n2_ready)
                    if step == "norm2_transpose" and s2:
                        keep_low(xt2, 3, None, xt2_hi, b2, xt2_lo)
                    if step == "router" and s2:
                        router(b2)
                    if step == "unit" and s3:
                        unit(k, b3)
                    if step == "down" and s3:
                        down(k, b3)
                assert not s1 or steps[chain1] == chain1.per_batch, steps[chain1]
                assert not s2 or steps[chain2] == chain2.per_batch, steps[chain2]

            v.memset(h0[:], 0.0).then_inc(s_clear, 1)
            v.memset(v_ones[:], 1.0)
            for j in range(RAW):
                w = slice(j * piece, (j + 1) * piece)
                dve.wait_ge(s_raw[j], 32)
                v.tensor_copy(wa_hi[:, w], raw_a[j]).then_inc(s_split, 1)
                v.tensor_copy(wb[:, w], raw_b[j]).then_inc(s_split, 1)
                dve.wait_ge(s_split, 4 * j + 2)
                v.tensor_tensor(wa_lo[:, w], raw_a[j], f32(wa_hi[:, w]), ALU.subtract).then_inc(s_split, 1)
                v.tensor_tensor(wb[REST:P, w], raw_b[j][REST:P], f32(wb[REST:P, w]), ALU.subtract).then_inc(s_split, 1)
            dve.wait_ge(s_down, 16)
            v.tensor_scalar(w_down_s[:], w_down_s[:], 0.5, None, ALU.mult).then_inc(s_halve, 1)
            dve.wait_ge(s_const, 16 * 10)
            dve.wait_ge(s_split, 4 * RAW)
            turns(dve, turn)


def kernel(x, txt, L0_tok_W_lin, L0_tok_b_lin, L0_tok_cls_token, L0_attn_qkv_w, L0_attn_c_proj_w,
           L0_ffn_shared_gate, L0_ffn_shared_up, L0_ffn_shared_down, L0_ffn_routed_gate, L0_ffn_routed_up,
           L0_ffn_routed_down, L0_ffn_router_w, L0_ffn_routing_bias):
    import numpy as np
    import concourse.bacc as bacc
    from concourse.bass_utils import run_bass_kernel_spmd

    x, txt = np.asarray(x), np.asarray(txt)
    xp = x.reshape(BATCH, CHANNELS, GRID, PATCH, GRID, PATCH).transpose(0, 1, 3, 5, 2, 4)
    xp = xp.reshape(BATCH, KT, P, PATCHES).transpose(0, 2, 1, 3)
    w_tok = np.asarray(L0_tok_W_lin).T.reshape(KT, P, DIM).transpose(1, 0, 2)
    qkv = np.asarray(L0_attn_qkv_w).transpose(2, 0, 1).reshape(DIM, 3 * DIM)
    proj = np.asarray(L0_attn_c_proj_w).T
    gates = [np.asarray(L0_ffn_shared_gate), *np.asarray(L0_ffn_routed_gate)]
    ups = [np.asarray(L0_ffn_shared_up), *np.asarray(L0_ffn_routed_up)]
    w = np.concatenate([qkv, proj, *[a for pair in zip(gates, ups) for a in pair]], axis=1)
    w_a, w_b = w[:P], np.concatenate([w[P:], w[P:]], axis=0)
    downs = np.concatenate([np.asarray(L0_ffn_shared_down)[None], np.asarray(L0_ffn_routed_down)], axis=0)
    w_down = downs.reshape(UNITS, P, DIM).transpose(1, 0, 2)

    row = np.arange(P)
    pos = np.stack([np.where(row < PATCHES0, row + 1, 0), REAL0 + row, REAL0 + P + row], axis=1).astype(np.float32)
    freqs = (np.float32(1.0 / 1024.0) ** np.linspace(0.0, 1.0, HEAD_DIM // 4, dtype=np.float32)).astype(np.float32)
    theta = pos[:, :, None] * freqs
    cos, sin = np.cos(theta).astype(np.float32), np.sin(theta).astype(np.float32)
    half_cos = np.concatenate([cos, np.ones_like(cos)], axis=2)
    rot_cos = np.concatenate([half_cos, half_cos], axis=2)
    rot_sin = np.concatenate([sin, -sin], axis=2)
    p0 = np.where(np.arange(COLS0) < PATCHES0, np.arange(COLS0) + 1, 0)
    mask0 = (p0[:REAL0, None] <= p0[None, :]).astype(np.float32)
    mask1 = np.triu(np.ones((P, P), np.float32))

    sent = {
        "xp": xp, "txt": txt, "w_tok": w_tok, "bias": np.asarray(L0_tok_b_lin).reshape(1, DIM),
        "cls": np.asarray(L0_tok_cls_token), "w_a": w_a, "w_b": w_b, "w_down": w_down,
        "w_router": np.asarray(L0_ffn_router_w).T.reshape(1, EXPERTS * DIM),
        "b_router": np.asarray(L0_ffn_routing_bias).reshape(1, EXPERTS),
        "rot_cos": rot_cos, "rot_sin": rot_sin, "mask0": mask0, "mask1": mask1,
        "identity": np.eye(P, dtype=np.float32),
    }
    nc = bacc.Bacc("TRN2", target_bir_lowering=False, num_devices=1)
    arrays, args = {}, {}
    for name, a in sent.items():
        a = np.ascontiguousarray(a)
        arrays[f"in_{name}"] = a
        args[name] = nc.dram_tensor(f"in_{name}", a.shape, mybir.dt.from_np(a.dtype), kind="ExternalInput").ap()
    for name in ("bias", "w_router", "b_router"):
        args[name] = args[name][0]
    out = nc.dram_tensor("out_0", (BATCH, TOKENS, DIM), F32, kind="ExternalOutput").ap()
    build(nc, out=out, **args)
    r = run_bass_kernel_spmd(nc, [arrays], core_ids=[0])
    return r.results[0]["out_0"]
```

```python
from contextlib import ExitStack

import concourse.bass as bass
from concourse import mybir

F32 = mybir.dt.float32
F32R = mybir.dt.float32r
I32 = mybir.dt.int32
ALU = mybir.AluOpType
ACT = mybir.ActivationFunctionType
AX_X = mybir.AxisListType.X

BATCH, CHANNELS, IMAGE = 32, 3, 224
GRID = 14
PATCH = IMAGE // GRID
PATCH_DIM = CHANNELS * PATCH * PATCH
PATCHES = GRID * GRID
TXT, DIM = 128, 192
HEADS, HEAD_DIM = 12, 16
EXPERTS, INNER = 3, 384
FFNS = EXPERTS + 1
TOKENS = 1 + PATCHES + TXT
LN_EPS, RMS_EPS, ATTN_SCALE = 1e-5, 1.1920928955078125e-07, 0.12
RSQRT_MAGIC = 0x5F3759DF

P = 128
KT = PATCH_DIM // P
TILES = 3
PATCHES0 = PATCHES - P
REAL0 = PATCHES0 + 1
COLS0 = REAL0 + 1
COLS = COLS0 + 2 * P
TILE_AT = [0, COLS0, COLS0 + P]
TILE_COLS = [COLS0, P, P]
QK = 2 * DIM
REST = DIM - P
WIDE = DIM + REST
PAIRS = HEADS // 2
GROUP = 4
GROUPS = HEADS // GROUP
SLOT = 32
P_COLS = COLS + 3 * P
W_QKV, W_PROJ, W_FFN = 0, 3 * DIM, 4 * DIM
W_ALL = W_FFN + FFNS * 2 * INNER
CHUNKS = INNER // P
UNITS = FFNS * CHUNKS

PE_ORDER = """
gate0 qk_turn0 qk_turn1 qk_turn2 qk_turn3 up0 embed0 qk_turn4 qk_turn5 gate1 embed1 qk_turn6
qk_turn7 qk_turn8 qk_turn9 up1 qk_turn10 qk_turn11 gate2 score_a0 score_b0 up2 score_a1 score_b1
score_a2 gate3 down0 score_b2 value0 score_b3 score_a3 up3 score_a4 gate4 down1 up4 score_b4
score_a5 gate5 up5 value1 score_b5 norm1_turn0 gate6 down2 norm1_turn1 up6 gate7 value2 up7
y_to_rows0 y_to_rows1 y_to_rows2 gate8 up8 down3 y_to_cols0 y_to_cols1 project_qk0 project_qk1
project_qk2 down4 project_y gate9 down5 up9 gate10 up10 gate11 project_v up11 norm2_turn0
norm2_turn1 down6 down7
""".split()
ACT_ORDER = """
q_keep0 q_keep1 residual tanh0 q_keep2 q_keep3 tanh1 q_keep4 q_keep5 exp_a0 tanh2 exp_b0 exp_a1
exp_b1 tanh3 exp_b2 exp_a2 exp_a3 exp_b3 norm1_apply tanh4 exp_a4 y_keep0 tanh5 exp_b4 exp_a5 exp_b5
norm1_hi0 y_keep1 tanh6 norm1_hi1 y_keep2 tanh7 tanh8 y_hi0 y_hi1 square tanh9 tanh10 norm2_apply
tanh11 v_keep0 v_keep1 norm2_hi0 norm2_hi1 qk_hi0 qk_hi1 router_exp
""".split()
DVE_ORDER = """
k_keep0 gate0 up0 k_keep1 k_keep2 h0 k_keep3 k_keep4 gate1 up1 k_keep5 gate2 up2 mask_a0 norm1_stats
mask_b0 mask_a1 mask_b1 gate3 norm1_newton0 norm1_newton1 mask_b2 sum0 norm1_newton2 up3 mask_a2
mask_b3 mask_a3 gate4 mask_a4 up4 gate5 sum1 up5 mask_b4 gate6 mask_a5 norm1_lo0 mask_b5 sum2 up6
norm1_lo1 gate7 up7 y_rows gate8 up8 sum3 y_lo0 y_lo1 rms_sum sum4 h1 rms_newton0 norm2_stats gate9
norm2_newton0 norm2_newton1 up9 norm2_newton2 rms_newton1 gate10 sum5 rms_newton2 up10 rotate0
gate11 rotate1 up11 norm2_lo0 lo_parts norm2_lo1 sum6 router_dot sum7 router_pick
""".split()


def named(step):
    name = step.rstrip("0123456789")
    return (name, int(step[len(name):] or 0)) if name != "h" else (step, 0)


class Signal:

    def __init__(self, sem, per_batch):
        self.sem, self.per_batch = sem, per_batch

    def at(self, batch, count):
        return self.per_batch * batch + count


def later(batch):
    return not (isinstance(batch, int) and batch == 0)


def build(nc, xp, txt, w_tok, bias, cls, w_a, w_b, w_down, w_router, b_router, rot_cos, rot_sin,
          mask0, mask1, identity, out):
    with ExitStack() as ctx:
        def sb(name, shape, dt=F32):
            return ctx.enter_context(nc.sbuf_tensor(name, shape, dt))

        def signal(name, per_batch):
            return Signal(ctx.enter_context(nc.semaphore(name)), per_batch)

        ident = sb("ident", [P, P])
        bias_rows = sb("bias_rows", [P, DIM])
        router_rows = sb("router_rows", [P, EXPERTS, DIM])
        router_bias = sb("router_bias", [P, EXPERTS])
        cos_t = sb("cos_t", [P, TILES, HEAD_DIM])
        sin_t = sb("sin_t", [P, TILES, HEAD_DIM // 2])
        causal0 = sb("causal0", [REAL0, COLS0])
        causal1 = sb("causal1", [P, P])
        w_tok_s = sb("w_tok_s", [P, KT, DIM])
        wa_hi = sb("wa_hi", [P, W_ALL], F32R)
        wa_lo = sb("wa_lo", [P, W_ALL], F32R)
        wb = sb("wb", [P, W_ALL], F32R)
        w_down_s = sb("w_down_s", [P, UNITS, DIM])
        x_s = sb("x_s", [P, KT, PATCHES])
        h0 = sb("h0", [P, TILES, DIM])
        stats = sb("stats", [P, TILES, 6])
        mean_var = sb("mean_var", [P, TILES, 2])
        rstd = sb("rstd", [P, 4, TILES])
        x_n = sb("x_n", [P, TILES, WIDE])
        xt = sb("xt", [P, 4, COLS], F32R)
        squares = sb("squares", [P, TILES * 2 * HEADS, HEAD_DIM])
        rms = sb("rms", [P, 4, TILES * 2 * HEADS])
        rotated = sb("rotated", [P, TILES * 2 * HEADS, HEAD_DIM])
        crossed = sb("crossed", [P, TILES, 2 * HEADS, HEAD_DIM // 2])
        normed = [sb(f"{a}_normed", [P, TILES * HEADS, HEAD_DIM]) for a in "qk"]
        qk_split = [sb(f"{a}_split", [P, TILES * HEADS, 4, HEAD_DIM], F32R) for a in "qk"]
        v_ones = sb("v_ones", [P, TILES, HEADS, SLOT])
        residual = sb("residual", [P, TILES, DIM])
        qt = sb("qt", [P, PAIRS, COLS], F32R)
        kt = sb("kt", [P, PAIRS, COLS], F32R)
        probs = sb("probs", [P, 2 * GROUP, P_COLS])
        y_cols = sb("y_cols", [P, GROUPS, COLS])
        row_sum = sb("row_sum", [P, TILES, HEADS])
        y_rows = sb("y_rows", [P, TILES, WIDE])
        yt = sb("yt", [P, 4, COLS], F32R)
        h1 = sb("h1", [P, TILES, DIM])
        stats2 = sb("stats2", [P, TILES, 6])
        mean_var2 = sb("mean_var2", [P, TILES, 2])
        rstd2 = sb("rstd2", [P, 4, TILES])
        x_n2 = sb("x_n2", [P, TILES, WIDE])
        xt2 = sb("xt2", [P, 4, COLS], F32R)
        junk = sb("junk", [P, TILES, EXPERTS, DIM])
        logit = sb("logit", [P, TILES, EXPERTS])
        route = sb("route", [P, 8, TILES, EXPERTS])
        tanh_g = sb("tanh_g", [P, COLS])
        gated = sb("gated", [P, COLS])
        ht = sb("ht", [P, 2, CHUNKS, COLS])
        o = sb("o", [P, TILES, DIM])

        ps = ctx.enter_context(nc.psum_tensor("ps", [P, 8, 512], F32))
        GATE, UP, DOWN = 5, 6, 7

        s_const = ctx.enter_context(nc.semaphore("constants_loaded"))
        RAW = 4
        s_raw = [ctx.enter_context(nc.semaphore(f"raw_weights_{j}_loaded")) for j in range(RAW)]
        s_down = ctx.enter_context(nc.semaphore("raw_down_loaded"))
        s_split = ctx.enter_context(nc.semaphore("weights_split"))
        s_clear = ctx.enter_context(nc.semaphore("buffers_cleared"))
        s_halve = ctx.enter_context(nc.semaphore("down_halved"))
        x_loaded = signal("x_loaded", 16)
        txt_loaded = signal("txt_loaded", 16)
        stored = signal("stored", 64)
        embedded = signal("embedded", 2)
        n1_turned = signal("n1_turned", 2)
        qk_done = signal("qk_done", 3)
        v_done = signal("v_done", 2)
        qk_turned = signal("qk_turned", 2 * PAIRS)
        score0_done = signal("score0_done", PAIRS)
        score1_done = signal("score1_done", PAIRS)
        value_done = signal("value_done", GROUPS)
        y_turned = signal("y_turned", TILES)
        yt_turned = signal("yt_turned", 2)
        proj_done = signal("proj_done", 2)
        n2_turned = signal("n2_turned", 2)
        gate_done = signal("gate_done", UNITS)
        up_done = signal("up_done", UNITS)
        down_done = signal("down_done", 2 * FFNS)
        res_kept = signal("res_kept", 1)
        n1_applied = signal("n1_applied", 1)
        xt_hi = signal("xt_hi", 2)
        squared = signal("squared", 1)
        qk_hi = signal("qk_hi", 2)
        v_kept = signal("v_kept", 2)
        qt_kept = signal("qt_kept", PAIRS)
        exp0_done = signal("exp0_done", PAIRS)
        exp1_done = signal("exp1_done", PAIRS)
        y_kept = signal("y_kept", GROUPS)
        yt_hi = signal("yt_hi", 2)
        n2_applied = signal("n2_applied", 1)
        xt2_hi = signal("xt2_hi", 2)
        tanh_done = signal("tanh_done", UNITS)
        exp_logit = signal("exp_logit", 1)
        h0_ready = signal("h0_ready", 2)
        n1_ready = signal("n1_ready", 1)
        xt_lo = signal("xt_lo", 2)
        rot_ready = signal("rot_ready", 2)
        qk_lo = signal("qk_lo", 2)
        kt_kept = signal("kt_kept", PAIRS)
        masked_a = signal("masked_a", PAIRS)
        masked_b = signal("masked_b", PAIRS)
        y_ready = signal("y_ready", 1)
        yt_lo = signal("yt_lo", 2)
        h1_ready = signal("h1_ready", 1)
        n2_ready = signal("n2_ready", 1)
        xt2_lo = signal("xt2_lo", 2)
        logit_ready = signal("logit_ready", 1)
        gate_used = signal("gate_used", UNITS)
        h_ready = signal("h_ready", UNITS)
        summed = signal("summed", 2 * FFNS)
        chain1 = signal("chain1", 31)
        chain2 = signal("chain2", 24)

        def shaped(view, dims, offset=0):
            return bass.AP(view.tensor, view.offset + offset, [list(view.ap[0]), *dims])

        def f32(view):
            return view.bitcast(F32)

        def hi_lo(a, part):
            first, step = ((0, 2), (0, 3))[a] if part == 0 else ((1, 2), (1, 1))[a]
            return shaped(qk_split[a][:], [[4 * HEAD_DIM, TILES * HEADS], [step * HEAD_DIM, 2], [1, HEAD_DIM]],
                          first * HEAD_DIM)

        piece = W_ALL // RAW
        raw = probs[:, :, :].rearrange("p a b -> p (a b)")
        raw_a = [raw[:, (2 * (j % 2)) * piece:(2 * (j % 2) + 1) * piece] for j in range(RAW)]
        raw_b = [raw[:, (2 * (j % 2) + 1) * piece:(2 * (j % 2) + 2) * piece] for j in range(RAW)]

        block = ctx.enter_context(nc.Block())

        def turns(engine, turn):
            turn(-1, True, False, False)
            turn(0, True, True, False)
            turn(1, True, True, True)
            with engine.Fori(2, BATCH - 1) as i:
                turn(i, True, True, True)
            turn(BATCH - 1, False, True, True)
            turn(BATCH, False, False, True)

        @block.sync
        def _(sp):
            sp.dma_start(w_tok_s[:], w_tok).then_inc(s_const, 16)
            sp.dma_start(x_s[:], xp[0]).then_inc(x_loaded.sem, 16)
            sp.dma_start(bias_rows[:], bias.partition_broadcast(P)).then_inc(s_const, 16)
            sp.wait_ge(s_clear, 1)
            sp.dma_start(h0[REAL0 - 1:REAL0, 0, :], cls).then_inc(s_const, 16)
            sp.dma_start(h0[:, 2, :], txt[0]).then_inc(txt_loaded.sem, 16)
            sp.dma_start(ident[:], identity).then_inc(s_const, 16)
            sp.dma_start(cos_t[:], rot_cos).then_inc(s_const, 16)
            sp.dma_start(sin_t[:], rot_sin).then_inc(s_const, 16)
            sp.dma_start(causal0[:], mask0).then_inc(s_const, 16)
            sp.dma_start(causal1[:], mask1).then_inc(s_const, 16)
            sp.dma_start(router_rows[:].rearrange("p e d -> p (e d)"), w_router.partition_broadcast(P)).then_inc(s_const, 16)
            sp.dma_start(router_bias[:], b_router.partition_broadcast(P)).then_inc(s_const, 16)
            for j in range(RAW):
                if j >= 2:
                    sp.wait_ge(s_split, 4 * (j - 1))
                sp.dma_start(raw_a[j], w_a[:, j * piece:(j + 1) * piece]).then_inc(s_raw[j], 16)
                sp.dma_start(raw_b[j], w_b[:, j * piece:(j + 1) * piece]).then_inc(s_raw[j], 16)
            sp.dma_start(w_down_s[:], w_down).then_inc(s_down, 16)

            def turn(i, s1, s2, s3):
                b1, b2, b3 = i + 1, i, i - 1
                if s1 and s2:
                    sp.wait_ge(res_kept.sem, res_kept.at(b2, 1))
                    sp.wait_ge(n1_applied.sem, n1_applied.at(b2, 1))
                    sp.dma_start(h0[:, 2, :], txt[b1]).then_inc(txt_loaded.sem, 16)
                if s1 and not (isinstance(i, int) and b1 + 1 >= BATCH):
                    sp.wait_ge(embedded.sem, embedded.at(b1, 2))
                    sp.dma_start(x_s[:], xp[b1 + 1]).then_inc(x_loaded.sem, 16)
                if s3:
                    sp.wait_ge(summed.sem, summed.at(b3, 2 * FFNS))
                    sp.dma_start(out[b3, 1:REAL0, :], o[0:PATCHES0, 0, :]).then_inc(stored.sem, 16)
                    sp.dma_start(out[b3, 0:1, :], o[PATCHES0:REAL0, 0, :]).then_inc(stored.sem, 16)
                    sp.dma_start(out[b3, REAL0:REAL0 + P, :], o[:, 1, :]).then_inc(stored.sem, 16)
                    sp.dma_start(out[b3, REAL0 + P:TOKENS, :], o[:, 2, :]).then_inc(stored.sem, 16)

            turn(-1, True, False, False)
            turn(0, True, True, False)
            turn(1, True, True, True)
            with sp.Fori(2, BATCH - 2) as i:
                turn(i, True, True, True)
            turn(BATCH - 2, True, True, True)
            turn(BATCH - 1, False, True, True)
            turn(BATCH, False, False, True)
            sp.wait_ge(stored.sem, stored.at(BATCH - 1, 64))

        @block.tensor
        def _(pe):
            def mm(dst, lhs, rhs, first, last):
                return nc.tensor.matmul(dst, lhs, rhs, start=first, stop=last)

            def turned(dst, src):
                return nc.tensor.transpose(dst, src, ident[0:src.shape[0], 0:src.shape[0]])

            def tile_cols(t):
                return slice(TILE_AT[t], TILE_AT[t] + TILE_COLS[t])

            def row_cols(t):
                return slice(TILE_AT[t], TILE_AT[t] + P)

            def split_by_rows(dst, act_t, cols, w0, w1):
                w = slice(w0, w1)
                mm(dst, act_t[:, 0, cols], wa_hi[:, w], True, False)
                mm(dst, act_t[:, 0, cols], wa_lo[:, w], False, False)
                mm(dst, act_t[:, 1, cols], wa_hi[:, w], False, False)
                mm(dst, act_t[:, 2, cols], wb[:, w], False, False)
                return mm(dst, act_t[:, 3, cols], wb[:, w], False, True)

            def split_by_cols(dst, act_t, w0):
                w = slice(w0, w0 + P)
                mm(dst, wa_hi[:, w], act_t[:, 0, :], True, False)
                mm(dst, wa_hi[:, w], act_t[:, 1, :], False, False)
                mm(dst, wa_lo[:, w], act_t[:, 0, :], False, False)
                mm(dst, wb[:, w], act_t[:, 2, :], False, False)
                return mm(dst, wb[:, w], act_t[:, 3, :], False, True)

            def turn_rows(half, rows, bank, done):
                for t in range(TILES):
                    last = turned(ps[:, bank + half, tile_cols(t)], rows[0:TILE_COLS[t], t, half * P:half * P + P])
                last.then_inc(done.sem, 1)

            def qk_turn(n, b):
                m, bank = n // 2, n % 4
                if n == 0:
                    pe.wait_ge(qk_hi.sem, qk_hi.at(b, 2))
                    pe.wait_ge(qk_lo.sem, qk_lo.at(b, 2))
                    if later(b):
                        pe.wait_ge(xt2_hi.sem, xt2_hi.at(b - 1, 2))
                        pe.wait_ge(xt2_lo.sem, xt2_lo.at(b - 1, 2))
                if n >= 4:
                    kept = kt_kept if n % 2 else qt_kept
                    pe.wait_ge(kept.sem, kept.at(b, m - 1))
                for t in range(TILES):
                    heads = slice(t * HEADS + 2 * m, t * HEADS + 2 * m + 2)
                    x = f32(qk_split[n % 2][0:TILE_COLS[t], heads]).rearrange("p h s d -> p (h s d)")
                    last = turned(ps[:, bank, tile_cols(t)], x)
                last.then_inc(qk_turned.sem, 1)

            def embed(t, b):
                if t == 0:
                    pe.wait_ge(x_loaded.sem, x_loaded.at(b, 16))
                n = [PATCHES0, P][t]
                at = [0, PATCHES0][t]
                for j in range(KT):
                    last = mm(ps[0:n, 4, t * DIM:(t + 1) * DIM], x_s[:, j, at:at + n], w_tok_s[:, j, :], j == 0, j == KT - 1)
                last.then_inc(embedded.sem, 1)

            def score_a(p, b):
                if p == 0:
                    pe.wait_ge(qt_kept.sem, qt_kept.at(b, PAIRS))
                    pe.wait_ge(kt_kept.sem, kt_kept.at(b, PAIRS))
                else:
                    pe.wait_ge(exp0_done.sem, exp0_done.at(b, p))
                for j in range(2):
                    r = slice(64 * j, 64 * j + 64)
                    last = mm(ps[0:REAL0, j, 0:COLS], kt[r, p, 0:REAL0], qt[r, p, :], True, True)
                last.then_inc(score0_done.sem, 1)

            def score_b(p, b):
                if p:
                    pe.wait_ge(exp1_done.sem, exp1_done.at(b, p))
                else:
                    pe.wait_ge(qt_kept.sem, qt_kept.at(b, PAIRS))
                    pe.wait_ge(kt_kept.sem, kt_kept.at(b, PAIRS))
                for j in range(2):
                    r = slice(64 * j, 64 * j + 64)
                    mm(ps[:, 2 + j, 0:2 * P], kt[r, p, tile_cols(1)], qt[r, p, TILE_AT[1]:COLS], True, True)
                    last = mm(ps[:, 2 + j, 2 * P:3 * P], kt[r, p, tile_cols(2)], qt[r, p, tile_cols(2)], True, True)
                last.then_inc(score1_done.sem, 1)

            def value(g, b, s1):
                if g == 0:
                    pe.wait_ge(v_kept.sem, v_kept.at(b, 2))
                    if s1:
                        pe.wait_ge(h0_ready.sem, h0_ready.at(b + 1, 2))
                else:
                    pe.wait_ge(y_kept.sem, y_kept.at(b, g))
                pe.wait_ge(masked_a.sem, masked_a.at(b, 2 * g + 2))
                pe.wait_ge(masked_b.sem, masked_b.at(b, 2 * g + 2))
                base = GROUP * (g % 2)
                for t in range(TILES):
                    k = REAL0 if t == 0 else P
                    at = [0, COLS, COLS + 2 * P][t]
                    for j in range(GROUP):
                        last = mm(ps[SLOT * j:SLOT * j + SLOT, 4, TILE_AT[t]:COLS], v_ones[0:k, t, GROUP * g + j, :],
                                  probs[0:k, base + j, at:at + COLS - TILE_AT[t]], t == 0, t == TILES - 1)
                last.then_inc(value_done.sem, 1)

            def y_to_rows(t, b, s1):
                if t == 0:
                    pe.wait_ge(y_kept.sem, y_kept.at(b, GROUPS))
                    pe.wait_ge(exp0_done.sem, exp0_done.at(b, PAIRS))
                    pe.wait_ge(exp1_done.sem, exp1_done.at(b, PAIRS))
                    if s1:
                        pe.wait_ge(xt_hi.sem, xt_hi.at(b + 1, 2))
                        pe.wait_ge(xt_lo.sem, xt_lo.at(b + 1, 2))
                for g in range(GROUPS):
                    last = turned(ps[:, t, g * P:(g + 1) * P], y_cols[:, g, row_cols(t)])
                last.then_inc(y_turned.sem, 1)

            def project_qk(t, b, s2):
                if t == 0:
                    pe.wait_ge(xt_hi.sem, xt_hi.at(b, 2))
                    pe.wait_ge(xt_lo.sem, xt_lo.at(b, 2))
                    if s2:
                        pe.wait_ge(y_ready.sem, y_ready.at(b - 1, 1))
                split_by_rows(ps[:, t, 0:QK], xt, row_cols(t), W_QKV, W_QKV + QK).then_inc(qk_done.sem, 1)

            def project_v(b, s2):
                if s2:
                    if later(b):
                        pe.wait_ge(h1_ready.sem, h1_ready.at(b - 1, 1))
                for t in range(TILES):
                    last = split_by_rows(ps[:, 3 + t // 2, (t % 2) * DIM:(t % 2 + 1) * DIM], xt, row_cols(t),
                                         W_QKV + QK, W_QKV + 3 * DIM)
                    if t:
                        last.then_inc(v_done.sem, 1)

            def project_y(b):
                pe.wait_ge(yt_hi.sem, yt_hi.at(b, 2))
                pe.wait_ge(yt_lo.sem, yt_lo.at(b, 2))
                for t in range(TILES):
                    last = split_by_rows(ps[:, 3 + t // 2, (t % 2) * DIM:(t % 2 + 1) * DIM], yt, row_cols(t),
                                         W_PROJ, W_PROJ + DIM)
                    if t:
                        last.then_inc(proj_done.sem, 1)

            def gate(k, b):
                if k == 0:
                    pe.wait_ge(xt2_hi.sem, xt2_hi.at(b, 2))
                    pe.wait_ge(xt2_lo.sem, xt2_lo.at(b, 2))
                if k or later(b):
                    pe.wait_ge(gate_used.sem, gate_used.at(b, k))
                w = W_FFN + (k // CHUNKS) * 2 * INNER + (k % CHUNKS) * P
                split_by_cols(ps[:, GATE, 0:COLS], xt2, w).then_inc(gate_done.sem, 1)

            def up(k, b):
                if k == 0:
                    pe.wait_ge(xt2_hi.sem, xt2_hi.at(b, 2))
                    pe.wait_ge(xt2_lo.sem, xt2_lo.at(b, 2))
                if k or later(b):
                    pe.wait_ge(h_ready.sem, h_ready.at(b, k))
                w = W_FFN + (k // CHUNKS) * 2 * INNER + (k % CHUNKS) * P + INNER
                split_by_cols(ps[:, UP, 0:COLS], xt2, w).then_inc(up_done.sem, 1)

            def down(n, b):
                e = n // 2
                if n % 2 == 0:
                    pe.wait_ge(h_ready.sem, h_ready.at(b, CHUNKS * (e + 1)))
                if n or later(b):
                    pe.wait_ge(summed.sem, summed.at(b, n))
                for t in ([0, 1] if n % 2 == 0 else [2]):
                    for c in range(CHUNKS):
                        last = mm(ps[:, DOWN, (t % 2) * DIM:(t % 2 + 1) * DIM], ht[:, e % 2, c, row_cols(t)],
                                  w_down_s[:, CHUNKS * e + c, :], c == 0, c == CHUNKS - 1)
                last.then_inc(down_done.sem, 1)

            def turn(i, s1, s2, s3):
                b1, b2, b3 = i + 1, i, i - 1
                for name in PE_ORDER:
                    step, k = named(name)
                    if step == "qk_turn" and s2:
                        qk_turn(k, b2)
                    if step == "embed" and s1:
                        embed(k, b1)
                    if step == "score_a" and s2:
                        score_a(k, b2)
                    if step == "score_b" and s2:
                        score_b(k, b2)
                    if step == "value" and s2:
                        value(k, b2, s1)
                    if step == "norm1_turn" and s1:
                        pe.wait_ge(n1_applied.sem, n1_applied.at(b1, 1))
                        if s2:
                            pe.wait_ge(exp0_done.sem, exp0_done.at(b2, PAIRS))
                        turn_rows(k, x_n, 0, n1_turned)
                    if step == "y_to_rows" and s2:
                        y_to_rows(k, b2, s1)
                    if step == "y_to_cols" and s2:
                        pe.wait_ge(y_ready.sem, y_ready.at(b2, 1))
                        turn_rows(k, y_rows, 3, yt_turned)
                    if step == "project_y" and s2:
                        project_y(b2)
                    if step == "project_qk" and s1:
                        project_qk(k, b1, s2)
                    if step == "project_v" and s1:
                        project_v(b1, s2)
                    if step == "norm2_turn" and s2:
                        pe.wait_ge(n2_applied.sem, n2_applied.at(b2, 1))
                        if s1:
                            pe.wait_ge(v_kept.sem, v_kept.at(b1, 2))
                        turn_rows(k, x_n2, 3, n2_turned)
                    if step == "gate" and s3:
                        gate(k, b3)
                    if step == "up" and s3:
                        up(k, b3)
                    if step == "down" and s3:
                        down(k, b3)

            pe.wait_ge(s_const, 16 * 10)
            pe.wait_ge(s_split, 4 * RAW)
            pe.wait_ge(s_halve, 1)
            turns(pe, turn)

        @block.scalar
        def _(act):
            def copy(dst, src):
                return nc.scalar.activation(dst, src, ACT.Copy)

            def apply_norm(dst, src, coef):
                for t in range(TILES):
                    for a, z in ((0, 0), (P, REST)):
                        last = nc.scalar.activation(dst[:, t, a + z:DIM + z], src[:, t, a:DIM], ACT.Identity,
                                                    bias=coef[:, 3, t:t + 1], scale=coef[:, 0, t:t + 1])
                return last

            def turn(i, s1, s2, s3):
                b1, b2, b3 = i + 1, i, i - 1
                for name in ACT_ORDER:
                    step, k = named(name)
                    if step == "residual" and s2:
                        act.wait_ge(h0_ready.sem, h0_ready.at(b2, 2))
                        act.wait_ge(txt_loaded.sem, txt_loaded.at(b2, 16))
                        if later(b2):
                            act.wait_ge(h1_ready.sem, h1_ready.at(b2 - 1, 1))
                        copy(residual[:], h0[:]).then_inc(res_kept.sem, 1)
                    if step == "norm1_apply" and s1:
                        act.wait_ge(n1_ready.sem, n1_ready.at(b1, 1))
                        if later(b1):
                            act.wait_ge(n1_turned.sem, n1_turned.at(b1 - 1, 2))
                        apply_norm(x_n, h0, rstd).then_inc(n1_applied.sem, 1)
                    if step == "norm1_hi" and s1:
                        if later(b1):
                            act.wait_ge(v_done.sem, v_done.at(b1 - 1, 2))
                        act.wait_ge(n1_turned.sem, n1_turned.at(b1, k + 1))
                        copy(xt[:, 2 * k, :], ps[:, k, 0:COLS]).then_inc(xt_hi.sem, 1)
                    if step == "square" and s1:
                        act.wait_ge(qk_done.sem, qk_done.at(b1, TILES))
                        sq = squares[:].rearrange("p (t h) d -> p t (h d)", t=TILES)
                        nc.scalar.activation(sq, ps[:, 0:TILES, 0:QK], ACT.Square,
                                             scale=HEAD_DIM ** -0.5).then_inc(squared.sem, 1)
                    if step == "v_keep" and s1:
                        if later(b1):
                            act.wait_ge(value_done.sem, value_done.at(b1 - 1, GROUPS))
                        n = 2 - k
                        act.wait_ge(v_done.sem, v_done.at(b1, k + 1))
                        copy(v_ones[:, 2 * k:2 * k + n, :, 0:HEAD_DIM],
                             ps[:, 3 + k, 0:n * DIM].rearrange("p (t h d) -> p t h d", t=n, h=HEADS)).then_inc(v_kept.sem, 1)
                    if step == "qk_hi" and s1:
                        act.wait_ge(rot_ready.sem, rot_ready.at(b1, 2))
                        if later(b1):
                            act.wait_ge(qk_turned.sem, qk_turned.at(b1 - 1, 2 * PAIRS))
                        x = shaped(normed[k][:], [[HEAD_DIM, TILES * HEADS], [0, 2], [1, HEAD_DIM]])
                        copy(hi_lo(k, 0), x).then_inc(qk_hi.sem, 1)
                    if step == "q_keep" and s2:
                        if k == 0:
                            if later(b2):
                                act.wait_ge(score1_done.sem, score1_done.at(b2 - 1, PAIRS))
                        act.wait_ge(qk_turned.sem, qk_turned.at(b2, 2 * k + 1))
                        copy(qt[:, k, :], ps[:, (2 * k) % 4, 0:COLS]).then_inc(qt_kept.sem, 1)
                    slot = (2 * k) % (2 * GROUP)
                    if step in ("exp_a", "exp_b") and s2:
                        if k == 0 and later(b2):
                            act.wait_ge(value_done.sem, value_done.at(b2 - 1, GROUPS))
                        if k == 4:
                            act.wait_ge(value_done.sem, value_done.at(b2, 1))
                    if step == "exp_a" and s2:
                        act.wait_ge(score0_done.sem, score0_done.at(b2, k + 1))
                        nc.scalar.activation(probs[0:REAL0, slot:slot + 2, 0:COLS], ps[0:REAL0, 0:2, 0:COLS],
                                             ACT.Exp, scale=ATTN_SCALE).then_inc(exp0_done.sem, 1)
                    if step == "exp_b" and s2:
                        act.wait_ge(score1_done.sem, score1_done.at(b2, k + 1))
                        nc.scalar.activation(probs[:, slot:slot + 2, COLS:P_COLS], ps[:, 2:4, 0:3 * P],
                                             ACT.Exp, scale=ATTN_SCALE).then_inc(exp1_done.sem, 1)
                    if step == "y_keep" and s2:
                        if k == 0:
                            if later(b2):
                                act.wait_ge(y_turned.sem, y_turned.at(b2 - 1, TILES))
                        act.wait_ge(value_done.sem, value_done.at(b2, k + 1))
                        copy(y_cols[:, k, :], ps[:, 4, 0:COLS]).then_inc(y_kept.sem, 1)
                    if step == "y_hi" and s2:
                        if later(b2):
                            act.wait_ge(proj_done.sem, proj_done.at(b2 - 1, 2))
                        act.wait_ge(yt_turned.sem, yt_turned.at(b2, k + 1))
                        copy(yt[:, 2 * k, :], ps[:, 3 + k, 0:COLS]).then_inc(yt_hi.sem, 1)
                    if step == "norm2_apply" and s2:
                        act.wait_ge(n2_ready.sem, n2_ready.at(b2, 1))
                        if later(b2):
                            act.wait_ge(n2_turned.sem, n2_turned.at(b2 - 1, 2))
                        apply_norm(x_n2, h1, rstd2).then_inc(n2_applied.sem, 1)
                    if step == "norm2_hi" and s2:
                        if s3:
                            act.wait_ge(up_done.sem, up_done.at(b3, UNITS))
                        act.wait_ge(n2_turned.sem, n2_turned.at(b2, k + 1))
                        copy(xt2[:, 2 * k, :], ps[:, 3 + k, 0:COLS]).then_inc(xt2_hi.sem, 1)
                    if step == "router_exp" and s2:
                        act.wait_ge(logit_ready.sem, logit_ready.at(b2, 1))
                        nc.scalar.activation(route[:, 0], logit[:], ACT.Exp, scale=-1.0).then_inc(exp_logit.sem, 1)
                    if step == "tanh" and s3:
                        act.wait_ge(gate_done.sem, gate_done.at(b3, k + 1))
                        if k or later(b3):
                            act.wait_ge(gate_used.sem, gate_used.at(b3, k))
                        nc.scalar.activation(tanh_g[:], ps[:, GATE, 0:COLS], ACT.Tanh, scale=0.5).then_inc(tanh_done.sem, 1)

            turns(act, turn)

        @block.vector
        def _(dve):
            v = nc.vector
            steps = {chain1: 0, chain2: 0}

            def link(chain, instruction):
                steps[chain] += 1
                instruction.then_inc(chain.sem, 1)

            def chained(chain, b):
                if steps[chain] or later(b):
                    dve.wait_ge(chain.sem, chain.at(b, steps[chain]))

            def rsqrt_step(part, chain, b, x, y, tmp):
                if part == 0:
                    chained(chain, b)
                    link(chain, v.tensor_scalar(y.bitcast(I32), x.bitcast(I32), 1, None, ALU.logical_shift_right))
                    chained(chain, b)
                    link(chain, v.tensor_scalar(y.bitcast(I32), y.bitcast(I32), -1.0, float(RSQRT_MAGIC), ALU.mult, ALU.add))
                chained(chain, b)
                link(chain, v.tensor_tensor(tmp, y, y, ALU.mult))
                chained(chain, b)
                link(chain, v.scalar_tensor_tensor(out=tmp, in0=tmp, scalar=-0.5, in1=x, op0=ALU.mult, op1=ALU.mult))
                chained(chain, b)
                link(chain, v.scalar_tensor_tensor(out=y, in0=tmp, scalar=1.5, in1=y, op0=ALU.add, op1=ALU.mult))

            def norm_stats(chain, b, rows, st, mv, coef):
                for t in range(TILES):
                    last = v.bn_stats(st[:, t, :], rows[:, t, :])
                link(chain, last)
                chained(chain, b)
                v.tensor_copy(coef[:, 2, 0:1], st[:, 0, 0:1])
                for t in range(TILES):
                    last = v.bn_aggr(mv[:, t, :], st[:, t, :])
                link(chain, last)
                chained(chain, b)
                link(chain, v.tensor_scalar(coef[:, 1, :], mv[:, :, 1], LN_EPS, None, ALU.add))

            def norm_newton(part, chain, b, mv, coef, ready):
                rsqrt_step(part, chain, b, coef[:, 1, :], coef[:, 0, :], coef[:, 2, :])
                if part == 2:
                    chained(chain, b)
                    v.scalar_tensor_tensor(out=coef[:, 3, :], in0=mv[:, :, 0], scalar=-1.0, in1=coef[:, 0, :],
                                           op0=ALU.mult, op1=ALU.mult).then_inc(ready.sem, 1)

            def keep_low(h, dst, src_bank, hi_signal, b, lo_signal):
                dve.wait_ge(hi_signal.sem, hi_signal.at(b, h + 1))
                v.tensor_tensor(dst[:, 2 * h + 1, :], ps[:, src_bank + h, 0:COLS], f32(dst[:, 2 * h, :]),
                                ALU.subtract).then_inc(lo_signal.sem, 1)

            def rms_sum(b):
                dve.wait_ge(squared.sem, squared.at(b, 1))
                chained(chain1, b)
                link(chain1, v.tensor_reduce(rms[:, 1, :], squares[:], AX_X, ALU.add))
                chained(chain1, b)
                link(chain1, v.tensor_scalar(rms[:, 1, :], rms[:, 1, :], RMS_EPS, None, ALU.add))

            quarter, half = HEAD_DIM // 4, HEAD_DIM // 2

            def rotate(part, b):
                bank = ps[:, 0:TILES, 0:QK].rearrange("p t (h d) -> p t h d", h=2 * HEADS)
                rot = rotated[:].rearrange("p (t h) d -> p t h d", t=TILES)
                if part == 0:
                    dve.wait_ge(squared.sem, squared.at(b, 1))
                    chained(chain1, b)
                    c = shaped(cos_t[:], [[HEAD_DIM, TILES], [0, 2 * HEADS], [1, HEAD_DIM]])
                    v.tensor_tensor(rot, bank, c, ALU.mult)
                    for a in range(2):
                        s = shaped(sin_t[:, :, a * quarter:(a + 1) * quarter], [[half, TILES], [0, 2 * HEADS], [1, quarter]])
                        last = v.tensor_tensor(crossed[:, :, :, a * quarter:(a + 1) * quarter],
                                               bank[:, :, :, half * (1 - a):half * (1 - a) + quarter], s, ALU.mult)
                    link(chain1, last)
                if part == 1:
                    r = shaped(rotated[:], [[HEAD_DIM, TILES * 2 * HEADS], [half, 2], [1, quarter]])
                    cr = crossed[:].rearrange("p t h (a d) -> p (t h) a d", a=2)
                    chained(chain1, b)
                    link(chain1, v.tensor_tensor(r, r, cr, ALU.add))
                    if later(b):
                        dve.wait_ge(qk_hi.sem, qk_hi.at(b - 1, 2))
                    chained(chain1, b)
                    for a in range(2):
                        x = shaped(rotated[:], [[QK, TILES], [HEAD_DIM, HEADS], [1, HEAD_DIM]], a * DIM)
                        scale = shaped(rms[:, 0, :], [[2 * HEADS, TILES], [1, HEADS], [0, HEAD_DIM]], a * HEADS)
                        y = normed[a][:].rearrange("p (t h) d -> p t h d", t=TILES)
                        last = v.tensor_tensor(y, x, scale, ALU.mult)
                        last.then_inc(rot_ready.sem, 1)

            def lo_parts(b):
                if later(b):
                    dve.wait_ge(qk_turned.sem, qk_turned.at(b - 1, 2 * PAIRS))
                for a in range(2):
                    dve.wait_ge(qk_hi.sem, qk_hi.at(b, a + 1))
                    hi, lo = f32(hi_lo(a, 0)), hi_lo(a, 1)
                    link(chain1, v.tensor_tensor(lo[:, :, 0], normed[a][:], hi[:, :, 0], ALU.subtract))
                for a in range(2):
                    lo = hi_lo(a, 1)
                    chained(chain1, b)
                    v.tensor_copy(lo[:, :, 1], f32(lo[:, :, 0])).then_inc(qk_lo.sem, 1)

            def mask_a(p, b):
                slot = (2 * p) % (2 * GROUP)
                dve.wait_ge(exp0_done.sem, exp0_done.at(b, p + 1))
                d0 = probs[0:REAL0, slot:slot + 2, 0:COLS0]
                v.tensor_tensor(d0, d0, shaped(causal0[:], [[0, 2], [1, COLS0]]), ALU.mult).then_inc(masked_a.sem, 1)

            def mask_b(p, b):
                slot = (2 * p) % (2 * GROUP)
                dve.wait_ge(exp1_done.sem, exp1_done.at(b, p + 1))
                d1 = probs[:, slot:slot + 2, COLS:P_COLS]
                d1 = shaped(d1, [[P_COLS, 2], [2 * P, 2], [1, P]])
                v.tensor_tensor(d1, d1, shaped(causal1[:], [[0, 2], [0, 2], [1, P]]), ALU.mult).then_inc(masked_b.sem, 1)

            def router_dot(b):
                dve.wait_ge(n2_applied.sem, n2_applied.at(b, 1))
                chained(chain2, b)
                for t in range(TILES):
                    for e in range(EXPERTS):
                        last = v.tensor_tensor_reduce(junk[:, t, e, :], x_n2[:, t, 0:DIM], router_rows[:, e, :], 1.0, 0.0,
                                                      ALU.mult, ALU.add, route[:, 1, t, e:e + 1])
                link(chain2, last)
                bias3 = shaped(router_bias[:], [[0, TILES], [1, EXPERTS]])
                chained(chain2, b)
                v.tensor_tensor(logit[:], route[:, 1], bias3, ALU.add).then_inc(logit_ready.sem, 1)

            def router_pick(b):
                dve.wait_ge(exp_logit.sem, exp_logit.at(b, 1))
                link(chain2, v.tensor_scalar(route[:, 1], route[:, 0], 1.0, None, ALU.add))
                chained(chain2, b)
                link(chain2, v.reciprocal(route[:, 2], route[:, 1]))
                s = [route[:, 2, :, e] for e in range(EXPERTS)]
                keep = [route[:, 3, :, e] for e in range(EXPERTS)]
                m = [route[:, 4, :, e] for e in range(EXPERTS)]
                chained(chain2, b)
                v.tensor_tensor(m[0], s[1], s[2], ALU.min)
                v.tensor_tensor(m[1], s[1], s[0], ALU.is_gt)
                v.tensor_tensor(m[2], s[0], s[1], ALU.min)
                link(chain2, v.tensor_tensor(keep[1], s[1], s[2], ALU.is_ge))
                chained(chain2, b)
                v.tensor_tensor(keep[0], s[0], m[0], ALU.is_ge)
                v.tensor_tensor(keep[1], keep[1], m[1], ALU.max)
                link(chain2, v.tensor_tensor(keep[2], s[2], m[2], ALU.is_gt))
                chained(chain2, b)
                link(chain2, v.tensor_tensor(route[:, 5], route[:, 2], route[:, 3], ALU.mult))
                chained(chain2, b)
                link(chain2, v.tensor_reduce(route[:, 4, :, 0], route[:, 5], AX_X, ALU.add))
                chained(chain2, b)
                link(chain2, v.reciprocal(route[:, 4, :, 1], route[:, 4, :, 0]))
                total = shaped(route[:, 4, :, 1:2], [[EXPERTS, TILES], [0, EXPERTS]])
                chained(chain2, b)
                link(chain2, v.tensor_tensor(route[:, 6], route[:, 5], total, ALU.mult))

            def gate(k, b):
                if k or later(b):
                    dve.wait_ge(h_ready.sem, h_ready.at(b, k))
                dve.wait_ge(tanh_done.sem, tanh_done.at(b, k + 1))
                v.scalar_tensor_tensor(out=gated[:], in0=tanh_g[:], scalar=1.0, in1=ps[:, GATE, 0:COLS],
                                       op0=ALU.add, op1=ALU.mult).then_inc(gate_used.sem, 1)

            def up(k, b):
                dve.wait_ge(up_done.sem, up_done.at(b, k + 1))
                dve.wait_ge(gate_used.sem, gate_used.at(b, k + 1))
                v.tensor_tensor(ht[:, (k // CHUNKS) % 2, k % CHUNKS, :], gated[:], ps[:, UP, 0:COLS],
                                ALU.mult).then_inc(h_ready.sem, 1)

            def sum_up(n, b):
                e = n // 2
                dve.wait_ge(down_done.sem, down_done.at(b, n + 1))
                if n == 0:
                    if later(b):
                        dve.wait_ge(stored.sem, stored.at(b - 1, 64))
                tiles = [0, 1] if n % 2 == 0 else [2]
                if e:
                    dve.wait_ge(summed.sem, summed.at(b, n - 1))
                for t in tiles:
                    d = ps[:, DOWN, (t % 2) * DIM:(t % 2 + 1) * DIM]
                    if e == 0:
                        last = v.tensor_tensor(o[:, t, :], d, h1[:, t, :], ALU.add)
                    else:
                        last = v.scalar_tensor_tensor(out=o[:, t, :], in0=d, scalar=route[:, 6, t, e - 1:e],
                                                      in1=o[:, t, :], op0=ALU.mult, op1=ALU.add)
                last.then_inc(summed.sem, 1)

            def turn(i, s1, s2, s3):
                b1, b2, b3 = i + 1, i, i - 1
                steps[chain1] = steps[chain2] = 0
                for name in DVE_ORDER:
                    step, k = named(name)
                    if step == "k_keep" and s2:
                        if k == 0:
                            if later(b2):
                                dve.wait_ge(score1_done.sem, score1_done.at(b2 - 1, PAIRS))
                        dve.wait_ge(qk_turned.sem, qk_turned.at(b2, 2 * k + 2))
                        v.tensor_copy(kt[:, k, :], ps[:, (2 * k + 1) % 4, 0:COLS]).then_inc(kt_kept.sem, 1)
                    if step == "h0" and s1:
                        dve.wait_ge(embedded.sem, embedded.at(b1, 2))
                        if s2:
                            dve.wait_ge(res_kept.sem, res_kept.at(b2, 1))
                        for t, n in enumerate((PATCHES0, P)):
                            v.tensor_tensor(h0[0:n, t, :], ps[0:n, 4, t * DIM:(t + 1) * DIM], bias_rows[0:n, :],
                                            ALU.add).then_inc(h0_ready.sem, 1)
                    if step == "norm1_stats" and s1:
                        dve.wait_ge(txt_loaded.sem, txt_loaded.at(b1, 16))
                        dve.wait_ge(h0_ready.sem, h0_ready.at(b1, 2))
                        if later(b1):
                            dve.wait_ge(n1_applied.sem, n1_applied.at(b1 - 1, 1))
                        norm_stats(chain1, b1, h0, stats, mean_var, rstd)
                    if step == "norm1_newton" and s1:
                        norm_newton(k, chain1, b1, mean_var, rstd, n1_ready)
                    if step == "norm1_lo" and s1:
                        keep_low(k, xt, 0, xt_hi, b1, xt_lo)
                    if step == "rms_sum" and s1:
                        rms_sum(b1)
                    if step == "rms_newton" and s1:
                        rsqrt_step(k, chain1, b1, rms[:, 1, :], rms[:, 0, :], rms[:, 2, :])
                    if step == "rotate" and s1:
                        rotate(k, b1)
                    if step == "lo_parts" and s1:
                        lo_parts(b1)
                    if step == "mask_a" and s2:
                        mask_a(k, b2)
                    if step == "mask_b" and s2:
                        mask_b(k, b2)
                    if step == "y_rows" and s2:
                        dve.wait_ge(y_turned.sem, y_turned.at(b2, TILES))
                        yr = ps[:, 0:TILES, 0:QK].rearrange("p t (h s) -> p t h s", h=HEADS)
                        link(chain2, v.reciprocal(row_sum[:], yr[:, :, :, HEAD_DIM]))
                        if later(b2):
                            dve.wait_ge(yt_turned.sem, yt_turned.at(b2 - 1, 2))
                        chained(chain2, b2)
                        for at, first in ((0, 0), (DIM, P // HEAD_DIM)):
                            n = HEADS - first
                            last = v.tensor_tensor(shaped(y_rows[:], [[WIDE, TILES], [HEAD_DIM, n], [1, HEAD_DIM]], at),
                                                   yr[:, :, first:HEADS, 0:HEAD_DIM],
                                                   shaped(row_sum[:], [[HEADS, TILES], [1, n], [0, HEAD_DIM]], first),
                                                   ALU.mult)
                        last.then_inc(y_ready.sem, 1)
                    if step == "y_lo" and s2:
                        keep_low(k, yt, 3, yt_hi, b2, yt_lo)
                    if step == "h1" and s2:
                        for h, n in enumerate((2, 1)):
                            dve.wait_ge(proj_done.sem, proj_done.at(b2, h + 1))
                            dve.wait_ge(res_kept.sem, res_kept.at(b2, 1))
                            last = v.tensor_tensor(h1[:, 2 * h:2 * h + n, :],
                                                   ps[:, 3 + h, 0:n * DIM].rearrange("p (t d) -> p t d", t=n),
                                                   residual[:, 2 * h:2 * h + n, :], ALU.add)
                        last.then_inc(h1_ready.sem, 1)
                    if step == "norm2_stats" and s2:
                        dve.wait_ge(h1_ready.sem, h1_ready.at(b2, 1))
                        if later(b2):
                            dve.wait_ge(n2_applied.sem, n2_applied.at(b2 - 1, 1))
                        norm_stats(chain2, b2, h1, stats2, mean_var2, rstd2)
                    if step == "norm2_newton" and s2:
                        norm_newton(k, chain2, b2, mean_var2, rstd2, n2_ready)
                    if step == "norm2_lo" and s2:
                        keep_low(k, xt2, 3, xt2_hi, b2, xt2_lo)
                    if step == "router_dot" and s2:
                        router_dot(b2)
                    if step == "router_pick" and s2:
                        router_pick(b2)
                    if step == "gate" and s3:
                        gate(k, b3)
                    if step == "up" and s3:
                        up(k, b3)
                    if step == "sum" and s3:
                        sum_up(k, b3)
                assert not s1 or steps[chain1] == chain1.per_batch, steps[chain1]
                assert not s2 or steps[chain2] == chain2.per_batch, steps[chain2]

            v.memset(h0[:], 0.0).then_inc(s_clear, 1)
            v.memset(v_ones[:], 1.0)
            for j in range(RAW):
                w = slice(j * piece, (j + 1) * piece)
                dve.wait_ge(s_raw[j], 32)
                v.tensor_copy(wa_hi[:, w], raw_a[j]).then_inc(s_split, 1)
                v.tensor_copy(wb[:, w], raw_b[j]).then_inc(s_split, 1)
                dve.wait_ge(s_split, 4 * j + 2)
                v.tensor_tensor(wa_lo[:, w], raw_a[j], f32(wa_hi[:, w]), ALU.subtract).then_inc(s_split, 1)
                v.tensor_tensor(wb[REST:P, w], raw_b[j][REST:P], f32(wb[REST:P, w]), ALU.subtract).then_inc(s_split, 1)
            dve.wait_ge(s_down, 16)
            v.tensor_scalar(w_down_s[:], w_down_s[:], 0.5, None, ALU.mult).then_inc(s_halve, 1)
            dve.wait_ge(s_const, 16 * 10)
            dve.wait_ge(s_split, 4 * RAW)
            turns(dve, turn)


def kernel(x, txt, L0_tok_W_lin, L0_tok_b_lin, L0_tok_cls_token, L0_attn_qkv_w, L0_attn_c_proj_w,
           L0_ffn_shared_gate, L0_ffn_shared_up, L0_ffn_shared_down, L0_ffn_routed_gate, L0_ffn_routed_up,
           L0_ffn_routed_down, L0_ffn_router_w, L0_ffn_routing_bias):
    import numpy as np
    import concourse.bacc as bacc
    from concourse.bass_utils import run_bass_kernel_spmd

    x, txt = np.asarray(x), np.asarray(txt)
    xp = x.reshape(BATCH, CHANNELS, GRID, PATCH, GRID, PATCH).transpose(0, 1, 3, 5, 2, 4)
    xp = xp.reshape(BATCH, KT, P, PATCHES).transpose(0, 2, 1, 3)
    w_tok = np.asarray(L0_tok_W_lin).T.reshape(KT, P, DIM).transpose(1, 0, 2)
    qkv = np.asarray(L0_attn_qkv_w).transpose(2, 0, 1).reshape(DIM, 3 * DIM)
    proj = np.asarray(L0_attn_c_proj_w).T
    gates = [np.asarray(L0_ffn_shared_gate), *np.asarray(L0_ffn_routed_gate)]
    ups = [np.asarray(L0_ffn_shared_up), *np.asarray(L0_ffn_routed_up)]
    w = np.concatenate([qkv, proj, *[a for pair in zip(gates, ups) for a in pair]], axis=1)
    w_a, w_b = w[:P], np.concatenate([w[P:], w[P:]], axis=0)
    downs = np.concatenate([np.asarray(L0_ffn_shared_down)[None], np.asarray(L0_ffn_routed_down)], axis=0)
    w_down = downs.reshape(UNITS, P, DIM).transpose(1, 0, 2)

    row = np.arange(P)
    pos = np.stack([np.where(row < PATCHES0, row + 1, 0), REAL0 + row, REAL0 + P + row], axis=1).astype(np.float32)
    freqs = (np.float32(1.0 / 1024.0) ** np.linspace(0.0, 1.0, HEAD_DIM // 4, dtype=np.float32)).astype(np.float32)
    theta = pos[:, :, None] * freqs
    cos, sin = np.cos(theta).astype(np.float32), np.sin(theta).astype(np.float32)
    half_cos = np.concatenate([cos, np.ones_like(cos)], axis=2)
    rot_cos = np.concatenate([half_cos, half_cos], axis=2)
    rot_sin = np.concatenate([sin, -sin], axis=2)
    p0 = np.where(np.arange(COLS0) < PATCHES0, np.arange(COLS0) + 1, 0)
    mask0 = (p0[:REAL0, None] <= p0[None, :]).astype(np.float32)
    mask1 = np.triu(np.ones((P, P), np.float32))

    sent = {
        "xp": xp, "txt": txt, "w_tok": w_tok, "bias": np.asarray(L0_tok_b_lin).reshape(1, DIM),
        "cls": np.asarray(L0_tok_cls_token), "w_a": w_a, "w_b": w_b, "w_down": w_down,
        "w_router": np.asarray(L0_ffn_router_w).T.reshape(1, EXPERTS * DIM),
        "b_router": np.asarray(L0_ffn_routing_bias).reshape(1, EXPERTS),
        "rot_cos": rot_cos, "rot_sin": rot_sin, "mask0": mask0, "mask1": mask1,
        "identity": np.eye(P, dtype=np.float32),
    }
    nc = bacc.Bacc("TRN2", target_bir_lowering=False, num_devices=1)
    arrays, args = {}, {}
    for name, a in sent.items():
        a = np.ascontiguousarray(a)
        arrays[f"in_{name}"] = a
        args[name] = nc.dram_tensor(f"in_{name}", a.shape, mybir.dt.from_np(a.dtype), kind="ExternalInput").ap()
    for name in ("bias", "w_router", "b_router"):
        args[name] = args[name][0]
    out = nc.dram_tensor("out_0", (BATCH, TOKENS, DIM), F32, kind="ExternalOutput").ap()
    build(nc, out=out, **args)
    r = run_bass_kernel_spmd(nc, [arrays], core_ids=[0])
    return r.results[0]["out_0"]
```

```python
from contextlib import ExitStack

import concourse.bass as bass
from concourse import mybir

F32 = mybir.dt.float32
F32R = mybir.dt.float32r
I32 = mybir.dt.int32
ALU = mybir.AluOpType
ACT = mybir.ActivationFunctionType
AX_X = mybir.AxisListType.X

BATCH, CHANNELS, IMAGE = 32, 3, 224
GRID = 14
PATCH = IMAGE // GRID
PATCH_DIM = CHANNELS * PATCH * PATCH
PATCHES = GRID * GRID
TXT, DIM = 128, 192
HEADS, HEAD_DIM = 12, 16
EXPERTS, INNER = 3, 384
FFNS = EXPERTS + 1
TOKENS = 1 + PATCHES + TXT
LN_EPS, RMS_EPS, ATTN_SCALE = 1e-5, 1.1920928955078125e-07, 0.12
RSQRT_MAGIC = 0x5F3759DF
RSQRT_STEPS = 11

P = 128
KT = PATCH_DIM // P
TILES = 3
PATCHES0 = PATCHES - P
REAL0 = PATCHES0 + 1
COLS0 = REAL0 + 1
COLS = COLS0 + 2 * P
TILE_AT = [0, COLS0, COLS0 + P]
TILE_COLS = [COLS0, P, P]
QK = 2 * DIM
REST = DIM - P
WIDE = DIM + REST
PAIRS = HEADS // 2
GROUP = 4
GROUPS = HEADS // GROUP
SLOT = 32
P_COLS = COLS + 3 * P
W_QKV, W_PROJ, W_FFN = 0, 3 * DIM, 4 * DIM
W_ROUTER = W_FFN + FFNS * 2 * INNER
R_COLS = EXPERTS + EXPERTS % 2
W_ALL = W_ROUTER + R_COLS
CHUNKS = INNER // P
UNITS = FFNS * CHUNKS

PE_ORDER = """
gate0 qk_turn0 qk_turn1 embed0 qk_turn2 qk_turn3 up0 qk_turn4 qk_turn5 qk_turn6 gate1 qk_turn7
qk_turn8 qk_turn9 up1 qk_turn10 qk_turn11 gate2 score_a0 score_b0 up2 score_a1 embed1 score_b1
score_a2 gate3 score_b2 down0 score_b3 score_a3 value0 score_a4 up3 score_b4 gate4 up4 down1
score_a5 value1 gate5 score_b5 norm1_turn0 up5 gate6 norm1_turn1 up6 down2 gate7 value2 up7
y_to_rows0 y_to_rows1 y_to_rows2 gate8 up8 project_qk0 y_to_cols0 y_to_cols1 down3 project_qk1
project_qk2 down4 project_y gate9 up9 gate10 down5 up10 project_v gate11 up11 norm2_turn0
norm2_turn1 down6 router down7
""".split()
ACT_ORDER = """
q_keep0 residual q_keep1 tanh0 q_keep2 tanh1 q_keep3 q_keep4 q_keep5 exp_a0 exp_b0 tanh2 exp_a1
exp_b1 tanh3 exp_b2 exp_a2 exp_b3 exp_a3 norm1_apply tanh4 exp_a4 y_keep0 exp_b4 exp_a5 tanh5
y_keep1 tanh6 exp_b5 tanh7 norm1_hi0 norm1_hi1 y_keep2 tanh8 y_hi0 y_hi1 square tanh9 tanh10
norm2_apply tanh11 v_keep0 v_keep1 norm2_hi0 norm2_hi1 qk_hi0 qk_hi1 lo_copy0 lo_copy1 router_exp
""".split()
DVE_ORDER = """
k_keep0 gate0 k_keep1 k_keep2 up0 k_keep3 k_keep4 gate1 up1 k_keep5 gate2 h0 norm1_stats0 up2
norm1_stats1 norm1_stats2 norm1_newton0 norm1_newton1 norm1_newton2 norm1_newton3 norm1_newton4
norm1_newton5 norm1_newton6 norm1_newton7 norm1_newton8 gate3 sum0 norm1_newton9 norm1_newton10
norm1_newton11 up3 gate4 sum1 up4 gate5 up5 gate6 up6 sum2 norm1_lo0 norm1_lo1 gate7 up7 y_rows
gate8 up8 y_lo0 y_lo1 sum3 rms_sum0 sum4 rms_sum1 h1 rms_newton0 norm2_stats0 rms_newton1
norm2_stats1 rms_newton2 norm2_stats2 gate9 norm2_newton0 norm2_newton1 norm2_newton2 rms_newton3
norm2_newton3 norm2_newton4 rms_newton4 norm2_newton5 norm2_newton6 norm2_newton7 rms_newton5
norm2_newton8 up9 norm2_newton9 rms_newton6 norm2_newton10 sum5 norm2_newton11 gate10 rms_newton7
rotate0 rms_newton8 up10 rotate1 rms_newton9 gate11 rms_newton10 up11 rotate2 norm2_lo0 norm2_lo1
sum6 lo_part0 lo_part1 router_bias_add sum7 router_pick0 router_pick1 router_pick2 router_pick3
router_pick4 router_pick5 router_pick6 router_pick7
""".split()


def named(step):
    name = step.rstrip("0123456789")
    return (name, int(step[len(name):] or 0)) if name != "h" else (step, 0)


class Signal:

    def __init__(self, sem, per_batch):
        self.sem, self.per_batch = sem, per_batch

    def at(self, batch, count):
        return self.per_batch * batch + count


def later(batch):
    return not (isinstance(batch, int) and batch == 0)


def build(nc, xp, txt, w_tok, bias, cls, w_a, w_b, w_down, b_router, rot_cos, rot_sin,
          mask0, mask1, identity, out):
    with ExitStack() as ctx:
        def sb(name, shape, dt=F32):
            return ctx.enter_context(nc.sbuf_tensor(name, shape, dt))

        def signal(name, per_batch):
            return Signal(ctx.enter_context(nc.semaphore(name)), per_batch)

        ident = sb("ident", [P, P])
        ident_r = sb("ident_r", [P, P], F32R)
        bias_rows = sb("bias_rows", [P, DIM])
        router_bias = sb("router_bias", [P, EXPERTS])
        cos_t = sb("cos_t", [P, TILES, HEAD_DIM])
        sin_t = sb("sin_t", [P, TILES, HEAD_DIM // 2])
        causal0 = sb("causal0", [REAL0, COLS0])
        causal1 = sb("causal1", [P, P])
        w_tok_s = sb("w_tok_s", [P, KT, DIM])
        wa_hi = sb("wa_hi", [P, W_ALL], F32R)
        wa_lo = sb("wa_lo", [P, W_ALL], F32R)
        wb = sb("wb", [P, W_ALL], F32R)
        w_down_s = sb("w_down_s", [P, UNITS, DIM])
        x_s = sb("x_s", [P, KT, PATCHES])
        h0 = sb("h0", [P, TILES, DIM])
        stats = sb("stats", [P, TILES, 6])
        mean_var = sb("mean_var", [P, TILES, 2])
        rstd = sb("rstd", [P, 4, TILES])
        x_n = sb("x_n", [P, TILES, WIDE])
        xt = sb("xt", [P, 4, COLS], F32R)
        squares = sb("squares", [P, TILES * 2 * HEADS, HEAD_DIM])
        rms = sb("rms", [P, 4, TILES * 2 * HEADS])
        rotated = sb("rotated", [P, TILES * 2 * HEADS, HEAD_DIM])
        crossed = sb("crossed", [P, TILES, 2 * HEADS, HEAD_DIM // 2])
        normed = [sb(f"{a}_normed", [P, TILES * HEADS, HEAD_DIM]) for a in "qk"]
        qk_split = [sb(f"{a}_split", [P, TILES * HEADS, 4, HEAD_DIM], F32R) for a in "qk"]
        v_ones = sb("v_ones", [P, TILES, HEADS, SLOT])
        residual = sb("residual", [P, TILES, DIM])
        qt = sb("qt", [P, PAIRS, COLS], F32R)
        kt = sb("kt", [P, PAIRS, COLS], F32R)
        probs = sb("probs", [P, 2 * GROUP, P_COLS])
        y_cols = sb("y_cols", [P, GROUPS, COLS])
        row_sum = sb("row_sum", [P, TILES, HEADS])
        y_rows = sb("y_rows", [P, TILES, WIDE])
        yt = sb("yt", [P, 4, COLS], F32R)
        h1 = sb("h1", [P, TILES, DIM])
        stats2 = sb("stats2", [P, TILES, 6])
        mean_var2 = sb("mean_var2", [P, TILES, 2])
        rstd2 = sb("rstd2", [P, 4, TILES])
        x_n2 = sb("x_n2", [P, TILES, WIDE])
        xt2 = sb("xt2", [P, 4, COLS], F32R)
        logit = sb("logit", [P, TILES, EXPERTS])
        route = sb("route", [P, 8, TILES, EXPERTS])
        tanh_g = sb("tanh_g", [P, COLS])
        gated = sb("gated", [P, COLS])
        ht = sb("ht", [P, 2, CHUNKS, COLS])
        o = sb("o", [P, TILES, DIM])

        ps = ctx.enter_context(nc.psum_tensor("ps", [P, 8, 512], F32))
        GATE, UP, DOWN = 5, 6, 7

        s_const = ctx.enter_context(nc.semaphore("constants_loaded"))
        RAW = 4
        s_raw = [ctx.enter_context(nc.semaphore(f"raw_weights_{j}_loaded")) for j in range(RAW)]
        s_down = ctx.enter_context(nc.semaphore("raw_down_loaded"))
        s_split = ctx.enter_context(nc.semaphore("weights_split"))
        s_clear = ctx.enter_context(nc.semaphore("buffers_cleared"))
        s_halve = ctx.enter_context(nc.semaphore("down_halved"))
        x_loaded = signal("x_loaded", 16)
        txt_loaded = signal("txt_loaded", 16)
        stored = signal("stored", 64)
        embedded = signal("embedded", 2)
        n1_turned = signal("n1_turned", 2)
        qk_done = signal("qk_done", 3)
        v_done = signal("v_done", 2)
        qk_turned = signal("qk_turned", 2 * PAIRS)
        score0_done = signal("score0_done", PAIRS)
        score1_done = signal("score1_done", PAIRS)
        value_done = signal("value_done", GROUPS)
        y_turned = signal("y_turned", TILES)
        yt_turned = signal("yt_turned", 2)
        proj_done = signal("proj_done", 2)
        n2_turned = signal("n2_turned", 2)
        gate_done = signal("gate_done", UNITS)
        up_done = signal("up_done", UNITS)
        down_done = signal("down_done", 2 * FFNS)
        router_done = signal("router_done", 1)
        res_kept = signal("res_kept", 1)
        n1_applied = signal("n1_applied", 1)
        xt_hi = signal("xt_hi", 2)
        squared = signal("squared", 1)
        qk_hi = signal("qk_hi", 2)
        lo_copied = signal("lo_copied", 2)
        v_kept = signal("v_kept", 2)
        qt_kept = signal("qt_kept", PAIRS)
        exp0_done = signal("exp0_done", PAIRS)
        exp1_done = signal("exp1_done", PAIRS)
        y_kept = signal("y_kept", GROUPS)
        yt_hi = signal("yt_hi", 2)
        n2_applied = signal("n2_applied", 1)
        xt2_hi = signal("xt2_hi", 2)
        tanh_done = signal("tanh_done", UNITS)
        exp_logit = signal("exp_logit", 1)
        h0_ready = signal("h0_ready", 2)
        n1_ready = signal("n1_ready", 1)
        xt_lo = signal("xt_lo", 2)
        banks_read = signal("banks_read", 1)
        rot_added = signal("rot_added", 1)
        rot_ready = signal("rot_ready", 2)
        qk_lo = signal("qk_lo", 2)
        kt_kept = signal("kt_kept", PAIRS)
        masked_a = signal("masked_a", PAIRS)
        masked_b = signal("masked_b", PAIRS)
        y_ready = signal("y_ready", 1)
        yt_lo = signal("yt_lo", 2)
        h1_ready = signal("h1_ready", 1)
        n2_ready = signal("n2_ready", 1)
        xt2_lo = signal("xt2_lo", 2)
        logit_ready = signal("logit_ready", 1)
        gate_used = signal("gate_used", UNITS)
        h_ready = signal("h_ready", UNITS)
        summed = signal("summed", 2 * FFNS)
        chain1 = signal("chain1", 3 + RSQRT_STEPS + 2 + RSQRT_STEPS)
        chain2 = signal("chain2", 1 + 3 + RSQRT_STEPS + 8)

        def shaped(view, dims, offset=0):
            return bass.AP(view.tensor, view.offset + offset, [list(view.ap[0]), *dims])

        def f32(view):
            return view.bitcast(F32)

        def hi_lo(a, part):
            first, step = ((0, 2), (0, 3))[a] if part == 0 else ((1, 2), (1, 1))[a]
            return shaped(qk_split[a][:], [[4 * HEAD_DIM, TILES * HEADS], [step * HEAD_DIM, 2], [1, HEAD_DIM]],
                          first * HEAD_DIM)

        piece = W_ALL // RAW
        raw = probs[:, :, :].rearrange("p a b -> p (a b)")
        raw_a = [raw[:, (2 * (j % 2)) * piece:(2 * (j % 2) + 1) * piece] for j in range(RAW)]
        raw_b = [raw[:, (2 * (j % 2) + 1) * piece:(2 * (j % 2) + 2) * piece] for j in range(RAW)]

        block = ctx.enter_context(nc.Block())

        def turns(engine, turn):
            turn(-1, True, False, False)
            turn(0, True, True, False)
            turn(1, True, True, True)
            with engine.Fori(2, BATCH - 1) as i:
                turn(i, True, True, True)
            turn(BATCH - 1, False, True, True)
            turn(BATCH, False, False, True)

        @block.sync
        def _(sp):
            sp.dma_start(w_tok_s[:], w_tok).then_inc(s_const, 16)
            sp.dma_start(x_s[:], xp[0]).then_inc(x_loaded.sem, 16)
            sp.dma_start(bias_rows[:], bias.partition_broadcast(P)).then_inc(s_const, 16)
            sp.wait_ge(s_clear, 1)
            sp.dma_start(h0[REAL0 - 1:REAL0, 0, :], cls).then_inc(s_const, 16)
            sp.dma_start(h0[:, 2, :], txt[0]).then_inc(txt_loaded.sem, 16)
            sp.dma_start(ident[:], identity).then_inc(s_const, 16)
            sp.dma_start(cos_t[:], rot_cos).then_inc(s_const, 16)
            sp.dma_start(sin_t[:], rot_sin).then_inc(s_const, 16)
            sp.dma_start(causal0[:], mask0).then_inc(s_const, 16)
            sp.dma_start(causal1[:], mask1).then_inc(s_const, 16)
            sp.dma_start(router_bias[:], b_router.partition_broadcast(P)).then_inc(s_const, 16)
            for j in range(RAW):
                if j >= 2:
                    sp.wait_ge(s_split, 4 * (j - 1))
                sp.dma_start(raw_a[j], w_a[:, j * piece:(j + 1) * piece]).then_inc(s_raw[j], 16)
                sp.dma_start(raw_b[j], w_b[:, j * piece:(j + 1) * piece]).then_inc(s_raw[j], 16)
            sp.dma_start(w_down_s[:], w_down).then_inc(s_down, 16)

            def turn(i, s1, s2, s3):
                b1, b2, b3 = i + 1, i, i - 1
                if s1 and s2:
                    sp.wait_ge(res_kept.sem, res_kept.at(b2, 1))
                    sp.wait_ge(n1_applied.sem, n1_applied.at(b2, 1))
                    sp.dma_start(h0[:, 2, :], txt[b1]).then_inc(txt_loaded.sem, 16)
                if s1 and not (isinstance(i, int) and b1 + 1 >= BATCH):
                    sp.wait_ge(embedded.sem, embedded.at(b1, 2))
                    sp.dma_start(x_s[:], xp[b1 + 1]).then_inc(x_loaded.sem, 16)
                if s3:
                    sp.wait_ge(summed.sem, summed.at(b3, 2 * FFNS))
                    sp.dma_start(out[b3, 1:REAL0, :], o[0:PATCHES0, 0, :]).then_inc(stored.sem, 16)
                    sp.dma_start(out[b3, 0:1, :], o[PATCHES0:REAL0, 0, :]).then_inc(stored.sem, 16)
                    sp.dma_start(out[b3, REAL0:REAL0 + P, :], o[:, 1, :]).then_inc(stored.sem, 16)
                    sp.dma_start(out[b3, REAL0 + P:TOKENS, :], o[:, 2, :]).then_inc(stored.sem, 16)

            turn(-1, True, False, False)
            turn(0, True, True, False)
            turn(1, True, True, True)
            with sp.Fori(2, BATCH - 2) as i:
                turn(i, True, True, True)
            turn(BATCH - 2, True, True, True)
            turn(BATCH - 1, False, True, True)
            turn(BATCH, False, False, True)
            sp.wait_ge(stored.sem, stored.at(BATCH - 1, 64))

        @block.tensor
        def _(pe):
            def mm(dst, lhs, rhs, first, last):
                return nc.tensor.matmul(dst, lhs, rhs, start=first, stop=last)

            def turned(dst, src):
                return nc.tensor.transpose(dst, src, ident[0:src.shape[0], 0:src.shape[0]])

            def tile_cols(t):
                return slice(TILE_AT[t], TILE_AT[t] + TILE_COLS[t])

            def row_cols(t):
                return slice(TILE_AT[t], TILE_AT[t] + P)

            def split_by_rows(dst, act_t, cols, w0, w1):
                w = slice(w0, w1)
                mm(dst, act_t[:, 0, cols], wa_hi[:, w], True, False)
                mm(dst, act_t[:, 0, cols], wa_lo[:, w], False, False)
                mm(dst, act_t[:, 1, cols], wa_hi[:, w], False, False)
                mm(dst, act_t[:, 2, cols], wb[:, w], False, False)
                return mm(dst, act_t[:, 3, cols], wb[:, w], False, True)

            def split_by_cols(dst, act_t, w0):
                w = slice(w0, w0 + P)
                mm(dst, wa_hi[:, w], act_t[:, 0, :], True, False)
                mm(dst, wa_hi[:, w], act_t[:, 1, :], False, False)
                mm(dst, wa_lo[:, w], act_t[:, 0, :], False, False)
                mm(dst, wb[:, w], act_t[:, 2, :], False, False)
                return mm(dst, wb[:, w], act_t[:, 3, :], False, True)

            def turn_rows(half, rows, bank, done):
                for t in range(TILES):
                    last = turned(ps[:, bank + half, tile_cols(t)], rows[0:TILE_COLS[t], t, half * P:half * P + P])
                last.then_inc(done.sem, 1)

            def qk_turn(n, b):
                m, bank = n // 2, n % 4
                if n == 0:
                    pe.wait_ge(qk_hi.sem, qk_hi.at(b, 2))
                    pe.wait_ge(lo_copied.sem, lo_copied.at(b, 2))
                    if later(b):
                        pe.wait_ge(xt2_hi.sem, xt2_hi.at(b - 1, 2))
                        pe.wait_ge(xt2_lo.sem, xt2_lo.at(b - 1, 2))
                if n >= 4:
                    kept = kt_kept if n % 2 else qt_kept
                    pe.wait_ge(kept.sem, kept.at(b, m - 1))
                for t in range(TILES):
                    heads = slice(t * HEADS + 2 * m, t * HEADS + 2 * m + 2)
                    x = qk_split[n % 2][0:TILE_COLS[t], heads].rearrange("p h s d -> p (h s d)")
                    last = nc.tensor.transpose(ps[:, bank, tile_cols(t)].bitcast(F32R), x,
                                               ident_r[0:TILE_COLS[t], 0:TILE_COLS[t]])
                last.then_inc(qk_turned.sem, 1)

            def embed(t, b, s2):
                if t == 0:
                    pe.wait_ge(x_loaded.sem, x_loaded.at(b, 16))
                    if s2 and later(b - 1):
                        pe.wait_ge(logit_ready.sem, logit_ready.at(b - 2, 1))
                n = [PATCHES0, P][t]
                at = [0, PATCHES0][t]
                for j in range(KT):
                    last = mm(ps[0:n, 4, t * DIM:(t + 1) * DIM], x_s[:, j, at:at + n], w_tok_s[:, j, :], j == 0, j == KT - 1)
                last.then_inc(embedded.sem, 1)

            def score_a(p, b):
                if p == 0:
                    pe.wait_ge(qt_kept.sem, qt_kept.at(b, PAIRS))
                    pe.wait_ge(kt_kept.sem, kt_kept.at(b, PAIRS))
                else:
                    pe.wait_ge(exp0_done.sem, exp0_done.at(b, p))
                for j in range(2):
                    r = slice(64 * j, 64 * j + 64)
                    last = mm(ps[0:REAL0, j, 0:COLS], kt[r, p, 0:REAL0], qt[r, p, :], True, True)
                last.then_inc(score0_done.sem, 1)

            def score_b(p, b):
                if p:
                    pe.wait_ge(exp1_done.sem, exp1_done.at(b, p))
                else:
                    pe.wait_ge(qt_kept.sem, qt_kept.at(b, PAIRS))
                    pe.wait_ge(kt_kept.sem, kt_kept.at(b, PAIRS))
                for j in range(2):
                    r = slice(64 * j, 64 * j + 64)
                    mm(ps[:, 2 + j, 0:2 * P], kt[r, p, tile_cols(1)], qt[r, p, TILE_AT[1]:COLS], True, True)
                    last = mm(ps[:, 2 + j, 2 * P:3 * P], kt[r, p, tile_cols(2)], qt[r, p, tile_cols(2)], True, True)
                last.then_inc(score1_done.sem, 1)

            def value(g, b, s1):
                if g == 0:
                    pe.wait_ge(v_kept.sem, v_kept.at(b, 2))
                    if s1:
                        pe.wait_ge(h0_ready.sem, h0_ready.at(b + 1, 2))
                    else:
                        pe.wait_ge(logit_ready.sem, logit_ready.at(b - 1, 1))
                else:
                    pe.wait_ge(y_kept.sem, y_kept.at(b, g))
                pe.wait_ge(masked_a.sem, masked_a.at(b, 2 * g + 2))
                pe.wait_ge(masked_b.sem, masked_b.at(b, 2 * g + 2))
                base = GROUP * (g % 2)
                for t in range(TILES):
                    k = REAL0 if t == 0 else P
                    at = [0, COLS, COLS + 2 * P][t]
                    for j in range(GROUP):
                        last = mm(ps[SLOT * j:SLOT * j + SLOT, 4, TILE_AT[t]:COLS], v_ones[0:k, t, GROUP * g + j, :],
                                  probs[0:k, base + j, at:at + COLS - TILE_AT[t]], t == 0, t == TILES - 1)
                last.then_inc(value_done.sem, 1)

            def y_to_rows(t, b, s1):
                if t == 0:
                    pe.wait_ge(y_kept.sem, y_kept.at(b, GROUPS))
                    pe.wait_ge(exp0_done.sem, exp0_done.at(b, PAIRS))
                    pe.wait_ge(exp1_done.sem, exp1_done.at(b, PAIRS))
                    if s1:
                        pe.wait_ge(xt_hi.sem, xt_hi.at(b + 1, 2))
                        pe.wait_ge(xt_lo.sem, xt_lo.at(b + 1, 2))
                for g in range(GROUPS):
                    last = turned(ps[:, t, g * P:(g + 1) * P], y_cols[:, g, row_cols(t)])
                last.then_inc(y_turned.sem, 1)

            def project_qk(t, b, s2):
                if t == 0:
                    pe.wait_ge(xt_hi.sem, xt_hi.at(b, 2))
                    pe.wait_ge(xt_lo.sem, xt_lo.at(b, 2))
                    if s2:
                        pe.wait_ge(y_ready.sem, y_ready.at(b - 1, 1))
                split_by_rows(ps[:, t, 0:QK], xt, row_cols(t), W_QKV, W_QKV + QK).then_inc(qk_done.sem, 1)

            def project_v(b, s2):
                if s2:
                    if later(b):
                        pe.wait_ge(h1_ready.sem, h1_ready.at(b - 1, 1))
                for t in range(TILES):
                    last = split_by_rows(ps[:, 3 + t // 2, (t % 2) * DIM:(t % 2 + 1) * DIM], xt, row_cols(t),
                                         W_QKV + QK, W_QKV + 3 * DIM)
                    if t:
                        last.then_inc(v_done.sem, 1)

            def project_y(b):
                pe.wait_ge(yt_hi.sem, yt_hi.at(b, 2))
                pe.wait_ge(yt_lo.sem, yt_lo.at(b, 2))
                for t in range(TILES):
                    last = split_by_rows(ps[:, 3 + t // 2, (t % 2) * DIM:(t % 2 + 1) * DIM], yt, row_cols(t),
                                         W_PROJ, W_PROJ + DIM)
                    if t:
                        last.then_inc(proj_done.sem, 1)

            def router(b):
                pe.wait_ge(xt2_hi.sem, xt2_hi.at(b, 2))
                pe.wait_ge(xt2_lo.sem, xt2_lo.at(b, 2))
                for t in range(TILES):
                    last = split_by_rows(ps[:, 4, t * R_COLS:(t + 1) * R_COLS], xt2, row_cols(t), W_ROUTER, W_ALL)
                last.then_inc(router_done.sem, 1)

            def gate(k, b):
                if k == 0:
                    pe.wait_ge(xt2_hi.sem, xt2_hi.at(b, 2))
                    pe.wait_ge(xt2_lo.sem, xt2_lo.at(b, 2))
                if k or later(b):
                    pe.wait_ge(gate_used.sem, gate_used.at(b, k))
                w = W_FFN + (k // CHUNKS) * 2 * INNER + (k % CHUNKS) * P
                split_by_cols(ps[:, GATE, 0:COLS], xt2, w).then_inc(gate_done.sem, 1)

            def up(k, b):
                if k == 0:
                    pe.wait_ge(xt2_hi.sem, xt2_hi.at(b, 2))
                    pe.wait_ge(xt2_lo.sem, xt2_lo.at(b, 2))
                if k or later(b):
                    pe.wait_ge(h_ready.sem, h_ready.at(b, k))
                w = W_FFN + (k // CHUNKS) * 2 * INNER + (k % CHUNKS) * P + INNER
                split_by_cols(ps[:, UP, 0:COLS], xt2, w).then_inc(up_done.sem, 1)

            def down(n, b):
                e = n // 2
                if n % 2 == 0:
                    pe.wait_ge(h_ready.sem, h_ready.at(b, CHUNKS * (e + 1)))
                if n or later(b):
                    pe.wait_ge(summed.sem, summed.at(b, n))
                for t in ([0, 1] if n % 2 == 0 else [2]):
                    for c in range(CHUNKS):
                        last = mm(ps[:, DOWN, (t % 2) * DIM:(t % 2 + 1) * DIM], ht[:, e % 2, c, row_cols(t)],
                                  w_down_s[:, CHUNKS * e + c, :], c == 0, c == CHUNKS - 1)
                last.then_inc(down_done.sem, 1)

            def turn(i, s1, s2, s3):
                b1, b2, b3 = i + 1, i, i - 1
                for name in PE_ORDER:
                    step, k = named(name)
                    if step == "qk_turn" and s2:
                        qk_turn(k, b2)
                    if step == "embed" and s1:
                        embed(k, b1, s2)
                    if step == "score_a" and s2:
                        score_a(k, b2)
                    if step == "score_b" and s2:
                        score_b(k, b2)
                    if step == "value" and s2:
                        value(k, b2, s1)
                    if step == "norm1_turn" and s1:
                        pe.wait_ge(n1_applied.sem, n1_applied.at(b1, 1))
                        if s2:
                            pe.wait_ge(exp0_done.sem, exp0_done.at(b2, PAIRS))
                        turn_rows(k, x_n, 0, n1_turned)
                    if step == "y_to_rows" and s2:
                        y_to_rows(k, b2, s1)
                    if step == "y_to_cols" and s2:
                        pe.wait_ge(y_ready.sem, y_ready.at(b2, 1))
                        turn_rows(k, y_rows, 3, yt_turned)
                    if step == "project_y" and s2:
                        project_y(b2)
                    if step == "project_qk" and s1:
                        project_qk(k, b1, s2)
                    if step == "project_v" and s1:
                        project_v(b1, s2)
                    if step == "router" and s2:
                        router(b2)
                    if step == "norm2_turn" and s2:
                        pe.wait_ge(n2_applied.sem, n2_applied.at(b2, 1))
                        if s1:
                            pe.wait_ge(v_kept.sem, v_kept.at(b1, 2))
                        turn_rows(k, x_n2, 3, n2_turned)
                    if step == "gate" and s3:
                        gate(k, b3)
                    if step == "up" and s3:
                        up(k, b3)
                    if step == "down" and s3:
                        down(k, b3)

            pe.wait_ge(s_const, 16 * 9)
            pe.wait_ge(s_split, 4 * RAW)
            pe.wait_ge(s_halve, 2)
            turns(pe, turn)

        @block.scalar
        def _(act):
            def copy(dst, src):
                return nc.scalar.activation(dst, src, ACT.Copy)

            def apply_norm(dst, src, coef):
                for t in range(TILES):
                    for a, z in ((0, 0), (P, REST)):
                        last = nc.scalar.activation(dst[:, t, a + z:DIM + z], src[:, t, a:DIM], ACT.Identity,
                                                    bias=coef[:, 3, t:t + 1], scale=coef[:, 0, t:t + 1])
                return last

            def turn(i, s1, s2, s3):
                b1, b2, b3 = i + 1, i, i - 1
                for name in ACT_ORDER:
                    step, k = named(name)
                    if step == "residual" and s2:
                        act.wait_ge(h0_ready.sem, h0_ready.at(b2, 2))
                        act.wait_ge(txt_loaded.sem, txt_loaded.at(b2, 16))
                        if later(b2):
                            act.wait_ge(h1_ready.sem, h1_ready.at(b2 - 1, 1))
                        copy(residual[:], h0[:]).then_inc(res_kept.sem, 1)
                    if step == "norm1_apply" and s1:
                        act.wait_ge(n1_ready.sem, n1_ready.at(b1, 1))
                        if later(b1):
                            act.wait_ge(n1_turned.sem, n1_turned.at(b1 - 1, 2))
                        apply_norm(x_n, h0, rstd).then_inc(n1_applied.sem, 1)
                    if step == "norm1_hi" and s1:
                        if later(b1):
                            act.wait_ge(v_done.sem, v_done.at(b1 - 1, 2))
                        act.wait_ge(n1_turned.sem, n1_turned.at(b1, k + 1))
                        copy(xt[:, 2 * k, :], ps[:, k, 0:COLS]).then_inc(xt_hi.sem, 1)
                    if step == "square" and s1:
                        act.wait_ge(qk_done.sem, qk_done.at(b1, TILES))
                        sq = squares[:].rearrange("p (t h) d -> p t (h d)", t=TILES)
                        nc.scalar.activation(sq, ps[:, 0:TILES, 0:QK], ACT.Square,
                                             scale=HEAD_DIM ** -0.5).then_inc(squared.sem, 1)
                    if step == "v_keep" and s1:
                        if later(b1):
                            act.wait_ge(value_done.sem, value_done.at(b1 - 1, GROUPS))
                        n = 2 - k
                        act.wait_ge(v_done.sem, v_done.at(b1, k + 1))
                        copy(v_ones[:, 2 * k:2 * k + n, :, 0:HEAD_DIM],
                             ps[:, 3 + k, 0:n * DIM].rearrange("p (t h d) -> p t h d", t=n, h=HEADS)).then_inc(v_kept.sem, 1)
                    if step == "qk_hi" and s1:
                        act.wait_ge(rot_ready.sem, rot_ready.at(b1, 2))
                        if later(b1):
                            act.wait_ge(qk_turned.sem, qk_turned.at(b1 - 1, 2 * PAIRS))
                        x = shaped(normed[k][:], [[HEAD_DIM, TILES * HEADS], [0, 2], [1, HEAD_DIM]])
                        copy(hi_lo(k, 0), x).then_inc(qk_hi.sem, 1)
                    if step == "lo_copy" and s1:
                        act.wait_ge(qk_lo.sem, qk_lo.at(b1, k + 1))
                        lo = hi_lo(k, 1)
                        copy(lo[:, :, 1], f32(lo[:, :, 0])).then_inc(lo_copied.sem, 1)
                    if step == "q_keep" and s2:
                        if k == 0:
                            if later(b2):
                                act.wait_ge(score1_done.sem, score1_done.at(b2 - 1, PAIRS))
                        act.wait_ge(qk_turned.sem, qk_turned.at(b2, 2 * k + 1))
                        copy(qt[:, k, :], ps[:, (2 * k) % 4, 0:COLS]).then_inc(qt_kept.sem, 1)
                    slot = (2 * k) % (2 * GROUP)
                    if step in ("exp_a", "exp_b") and s2:
                        if k == 0 and later(b2):
                            act.wait_ge(value_done.sem, value_done.at(b2 - 1, GROUPS))
                        if k == 4:
                            act.wait_ge(value_done.sem, value_done.at(b2, 1))
                    if step == "exp_a" and s2:
                        act.wait_ge(score0_done.sem, score0_done.at(b2, k + 1))
                        nc.scalar.activation(probs[0:REAL0, slot:slot + 2, 0:COLS], ps[0:REAL0, 0:2, 0:COLS],
                                             ACT.Exp, scale=ATTN_SCALE).then_inc(exp0_done.sem, 1)
                    if step == "exp_b" and s2:
                        act.wait_ge(score1_done.sem, score1_done.at(b2, k + 1))
                        nc.scalar.activation(probs[:, slot:slot + 2, COLS:P_COLS], ps[:, 2:4, 0:3 * P],
                                             ACT.Exp, scale=ATTN_SCALE).then_inc(exp1_done.sem, 1)
                    if step == "y_keep" and s2:
                        if k == 0:
                            if later(b2):
                                act.wait_ge(y_turned.sem, y_turned.at(b2 - 1, TILES))
                        act.wait_ge(value_done.sem, value_done.at(b2, k + 1))
                        copy(y_cols[:, k, :], ps[:, 4, 0:COLS]).then_inc(y_kept.sem, 1)
                    if step == "y_hi" and s2:
                        if later(b2):
                            act.wait_ge(proj_done.sem, proj_done.at(b2 - 1, 2))
                        act.wait_ge(yt_turned.sem, yt_turned.at(b2, k + 1))
                        copy(yt[:, 2 * k, :], ps[:, 3 + k, 0:COLS]).then_inc(yt_hi.sem, 1)
                    if step == "norm2_apply" and s2:
                        act.wait_ge(n2_ready.sem, n2_ready.at(b2, 1))
                        if later(b2):
                            act.wait_ge(n2_turned.sem, n2_turned.at(b2 - 1, 2))
                        apply_norm(x_n2, h1, rstd2).then_inc(n2_applied.sem, 1)
                    if step == "norm2_hi" and s2:
                        if s3:
                            act.wait_ge(up_done.sem, up_done.at(b3, UNITS))
                        act.wait_ge(n2_turned.sem, n2_turned.at(b2, k + 1))
                        copy(xt2[:, 2 * k, :], ps[:, 3 + k, 0:COLS]).then_inc(xt2_hi.sem, 1)
                    if step == "router_exp" and s2:
                        act.wait_ge(logit_ready.sem, logit_ready.at(b2, 1))
                        nc.scalar.activation(route[:, 0], logit[:], ACT.Exp, scale=-1.0).then_inc(exp_logit.sem, 1)
                    if step == "tanh" and s3:
                        act.wait_ge(gate_done.sem, gate_done.at(b3, k + 1))
                        if k or later(b3):
                            act.wait_ge(gate_used.sem, gate_used.at(b3, k))
                        nc.scalar.activation(tanh_g[:], ps[:, GATE, 0:COLS], ACT.Tanh, scale=0.5).then_inc(tanh_done.sem, 1)

            turns(act, turn)

        @block.gpsimd
        def _(pool):
            def mask_a(p, b):
                slot = (2 * p) % (2 * GROUP)
                pool.wait_ge(exp0_done.sem, exp0_done.at(b, p + 1))
                d0 = probs[0:REAL0, slot:slot + 2, 0:COLS0]
                nc.gpsimd.tensor_tensor(d0, d0, shaped(causal0[:], [[0, 2], [1, COLS0]]), ALU.mult).then_inc(masked_a.sem, 1)

            def mask_b(p, b):
                slot = (2 * p) % (2 * GROUP)
                pool.wait_ge(exp1_done.sem, exp1_done.at(b, p + 1))
                d1 = probs[:, slot:slot + 2, COLS:P_COLS]
                d1 = shaped(d1, [[P_COLS, 2], [2 * P, 2], [1, P]])
                nc.gpsimd.tensor_tensor(d1, d1, shaped(causal1[:], [[0, 2], [0, 2], [1, P]]), ALU.mult).then_inc(masked_b.sem, 1)

            def turn(i, s1, s2, s3):
                if s2:
                    for p in range(PAIRS):
                        mask_a(p, i)
                        mask_b(p, i)

            turns(pool, turn)

        @block.vector
        def _(dve):
            v = nc.vector
            steps = {chain1: 0, chain2: 0}

            def link(chain, instruction):
                steps[chain] += 1
                instruction.then_inc(chain.sem, 1)

            def chained(chain, b):
                if steps[chain] or later(b):
                    dve.wait_ge(chain.sem, chain.at(b, steps[chain]))

            def rsqrt_step(n, chain, b, x, y, tmp):
                chained(chain, b)
                if n == 0:
                    link(chain, v.tensor_scalar(y.bitcast(I32), x.bitcast(I32), 1, None, ALU.logical_shift_right))
                elif n == 1:
                    link(chain, v.tensor_scalar(y.bitcast(I32), y.bitcast(I32), -1.0, float(RSQRT_MAGIC), ALU.mult, ALU.add))
                elif n % 3 == 2:
                    link(chain, v.tensor_tensor(tmp, y, y, ALU.mult))
                elif n % 3 == 0:
                    link(chain, v.scalar_tensor_tensor(out=tmp, in0=tmp, scalar=-0.5, in1=x, op0=ALU.mult, op1=ALU.mult))
                else:
                    link(chain, v.scalar_tensor_tensor(out=y, in0=tmp, scalar=1.5, in1=y, op0=ALU.add, op1=ALU.mult))

            def norm_stats(n, chain, b, st, mv, coef):
                chained(chain, b)
                if n == 1:
                    v.tensor_copy(coef[:, 2, 0:1], st[:, 0, 0:1])
                    for t in range(TILES):
                        last = v.bn_aggr(mv[:, t, :], st[:, t, :])
                    link(chain, last)
                else:
                    link(chain, v.tensor_scalar(coef[:, 1, :], mv[:, :, 1], LN_EPS, None, ALU.add))

            def norm_newton(n, chain, b, mv, coef, ready):
                if n < RSQRT_STEPS:
                    rsqrt_step(n, chain, b, coef[:, 1, :], coef[:, 0, :], coef[:, 2, :])
                else:
                    chained(chain, b)
                    v.scalar_tensor_tensor(out=coef[:, 3, :], in0=mv[:, :, 0], scalar=-1.0, in1=coef[:, 0, :],
                                           op0=ALU.mult, op1=ALU.mult).then_inc(ready.sem, 1)

            def keep_low(h, dst, src_bank, hi_signal, b, lo_signal):
                dve.wait_ge(hi_signal.sem, hi_signal.at(b, h + 1))
                v.tensor_tensor(dst[:, 2 * h + 1, :], ps[:, src_bank + h, 0:COLS], f32(dst[:, 2 * h, :]),
                                ALU.subtract).then_inc(lo_signal.sem, 1)

            def rms_sum(n, b):
                if n == 0:
                    dve.wait_ge(squared.sem, squared.at(b, 1))
                chained(chain1, b)
                if n == 0:
                    link(chain1, v.tensor_reduce(rms[:, 1, :], squares[:], AX_X, ALU.add))
                else:
                    link(chain1, v.tensor_scalar(rms[:, 1, :], rms[:, 1, :], RMS_EPS, None, ALU.add))

            quarter, half = HEAD_DIM // 4, HEAD_DIM // 2

            def rotate(part, b):
                bank = ps[:, 0:TILES, 0:QK].rearrange("p t (h d) -> p t h d", h=2 * HEADS)
                rot = rotated[:].rearrange("p (t h) d -> p t h d", t=TILES)
                if part == 0:
                    dve.wait_ge(squared.sem, squared.at(b, 1))
                    if later(b):
                        dve.wait_ge(rot_ready.sem, rot_ready.at(b - 1, 2))
                    c = shaped(cos_t[:], [[HEAD_DIM, TILES], [0, 2 * HEADS], [1, HEAD_DIM]])
                    v.tensor_tensor(rot, bank, c, ALU.mult)
                    for a in range(2):
                        s = shaped(sin_t[:, :, a * quarter:(a + 1) * quarter], [[half, TILES], [0, 2 * HEADS], [1, quarter]])
                        last = v.tensor_tensor(crossed[:, :, :, a * quarter:(a + 1) * quarter],
                                               bank[:, :, :, half * (1 - a):half * (1 - a) + quarter], s, ALU.mult)
                    last.then_inc(banks_read.sem, 1)
                if part == 1:
                    r = shaped(rotated[:], [[HEAD_DIM, TILES * 2 * HEADS], [half, 2], [1, quarter]])
                    cr = crossed[:].rearrange("p t h (a d) -> p (t h) a d", a=2)
                    dve.wait_ge(banks_read.sem, banks_read.at(b, 1))
                    v.tensor_tensor(r, r, cr, ALU.add).then_inc(rot_added.sem, 1)
                if part == 2:
                    dve.wait_ge(rot_added.sem, rot_added.at(b, 1))
                    if later(b):
                        dve.wait_ge(qk_hi.sem, qk_hi.at(b - 1, 2))
                    chained(chain1, b)
                    for a in range(2):
                        x = shaped(rotated[:], [[QK, TILES], [HEAD_DIM, HEADS], [1, HEAD_DIM]], a * DIM)
                        scale = shaped(rms[:, 0, :], [[2 * HEADS, TILES], [1, HEADS], [0, HEAD_DIM]], a * HEADS)
                        y = normed[a][:].rearrange("p (t h) d -> p t h d", t=TILES)
                        last = v.tensor_tensor(y, x, scale, ALU.mult)
                        last.then_inc(rot_ready.sem, 1)

            def lo_part(a, b):
                dve.wait_ge(qk_hi.sem, qk_hi.at(b, a + 1))
                hi, lo = f32(hi_lo(a, 0)), hi_lo(a, 1)
                v.tensor_tensor(lo[:, :, 0], normed[a][:], hi[:, :, 0], ALU.subtract).then_inc(qk_lo.sem, 1)

            def router_bias_add(b):
                bias3 = shaped(router_bias[:], [[0, TILES], [1, EXPERTS]])
                raw_logits = shaped(ps[:, 4, 0:1], [[R_COLS, TILES], [1, EXPERTS]])
                dve.wait_ge(router_done.sem, router_done.at(b, 1))
                v.tensor_tensor(logit[:], raw_logits, bias3, ALU.add).then_inc(logit_ready.sem, 1)

            def router_pick(n, b):
                s = [route[:, 2, :, e] for e in range(EXPERTS)]
                keep = [route[:, 3, :, e] for e in range(EXPERTS)]
                m = [route[:, 4, :, e] for e in range(EXPERTS)]
                if n == 0:
                    dve.wait_ge(exp_logit.sem, exp_logit.at(b, 1))
                    link(chain2, v.tensor_scalar(route[:, 1], route[:, 0], 1.0, None, ALU.add))
                    return
                chained(chain2, b)
                if n == 1:
                    link(chain2, v.reciprocal(route[:, 2], route[:, 1]))
                elif n == 2:
                    v.tensor_tensor(m[0], s[1], s[2], ALU.min)
                    v.tensor_tensor(m[1], s[1], s[0], ALU.is_gt)
                    v.tensor_tensor(m[2], s[0], s[1], ALU.min)
                    link(chain2, v.tensor_tensor(keep[1], s[1], s[2], ALU.is_ge))
                elif n == 3:
                    v.tensor_tensor(keep[0], s[0], m[0], ALU.is_ge)
                    v.tensor_tensor(keep[1], keep[1], m[1], ALU.max)
                    link(chain2, v.tensor_tensor(keep[2], s[2], m[2], ALU.is_gt))
                elif n == 4:
                    link(chain2, v.tensor_tensor(route[:, 5], route[:, 2], route[:, 3], ALU.mult))
                elif n == 5:
                    link(chain2, v.tensor_reduce(route[:, 4, :, 0], route[:, 5], AX_X, ALU.add))
                elif n == 6:
                    link(chain2, v.reciprocal(route[:, 4, :, 1], route[:, 4, :, 0]))
                else:
                    total = shaped(route[:, 4, :, 1:2], [[EXPERTS, TILES], [0, EXPERTS]])
                    link(chain2, v.tensor_tensor(route[:, 6], route[:, 5], total, ALU.mult))

            def gate(k, b):
                if k or later(b):
                    dve.wait_ge(h_ready.sem, h_ready.at(b, k))
                dve.wait_ge(tanh_done.sem, tanh_done.at(b, k + 1))
                v.scalar_tensor_tensor(out=gated[:], in0=tanh_g[:], scalar=1.0, in1=ps[:, GATE, 0:COLS],
                                       op0=ALU.add, op1=ALU.mult).then_inc(gate_used.sem, 1)

            def up(k, b):
                dve.wait_ge(up_done.sem, up_done.at(b, k + 1))
                dve.wait_ge(gate_used.sem, gate_used.at(b, k + 1))
                v.tensor_tensor(ht[:, (k // CHUNKS) % 2, k % CHUNKS, :], gated[:], ps[:, UP, 0:COLS],
                                ALU.mult).then_inc(h_ready.sem, 1)

            def sum_up(n, b):
                e = n // 2
                dve.wait_ge(down_done.sem, down_done.at(b, n + 1))
                if n == 0:
                    if later(b):
                        dve.wait_ge(stored.sem, stored.at(b - 1, 64))
                tiles = [0, 1] if n % 2 == 0 else [2]
                if e:
                    dve.wait_ge(summed.sem, summed.at(b, n - 1))
                for t in tiles:
                    d = ps[:, DOWN, (t % 2) * DIM:(t % 2 + 1) * DIM]
                    if e == 0:
                        last = v.tensor_tensor(o[:, t, :], d, h1[:, t, :], ALU.add)
                    else:
                        last = v.scalar_tensor_tensor(out=o[:, t, :], in0=d, scalar=route[:, 6, t, e - 1:e],
                                                      in1=o[:, t, :], op0=ALU.mult, op1=ALU.add)
                last.then_inc(summed.sem, 1)

            def turn(i, s1, s2, s3):
                b1, b2, b3 = i + 1, i, i - 1
                steps[chain1] = steps[chain2] = 0
                for name in DVE_ORDER:
                    step, k = named(name)
                    if step == "k_keep" and s2:
                        if k == 0:
                            if later(b2):
                                dve.wait_ge(score1_done.sem, score1_done.at(b2 - 1, PAIRS))
                        dve.wait_ge(qk_turned.sem, qk_turned.at(b2, 2 * k + 2))
                        v.tensor_copy(kt[:, k, :], ps[:, (2 * k + 1) % 4, 0:COLS]).then_inc(kt_kept.sem, 1)
                    if step == "h0" and s1:
                        dve.wait_ge(embedded.sem, embedded.at(b1, 2))
                        if s2:
                            dve.wait_ge(res_kept.sem, res_kept.at(b2, 1))
                        for t, n in enumerate((PATCHES0, P)):
                            v.tensor_tensor(h0[0:n, t, :], ps[0:n, 4, t * DIM:(t + 1) * DIM], bias_rows[0:n, :],
                                            ALU.add).then_inc(h0_ready.sem, 1)
                    if step == "norm1_stats" and s1 and k:
                        norm_stats(k, chain1, b1, stats, mean_var, rstd)
                    elif step == "norm1_stats" and s1:
                        dve.wait_ge(txt_loaded.sem, txt_loaded.at(b1, 16))
                        dve.wait_ge(h0_ready.sem, h0_ready.at(b1, 2))
                        if later(b1):
                            dve.wait_ge(n1_applied.sem, n1_applied.at(b1 - 1, 1))
                        for t in range(TILES):
                            last = v.bn_stats(stats[:, t, :], h0[:, t, :])
                        link(chain1, last)
                    if step == "norm1_newton" and s1:
                        norm_newton(k, chain1, b1, mean_var, rstd, n1_ready)
                    if step == "norm1_lo" and s1:
                        keep_low(k, xt, 0, xt_hi, b1, xt_lo)
                    if step == "rms_sum" and s1:
                        rms_sum(k, b1)
                    if step == "rms_newton" and s1:
                        rsqrt_step(k, chain1, b1, rms[:, 1, :], rms[:, 0, :], rms[:, 2, :])
                    if step == "rotate" and s1:
                        rotate(k, b1)
                    if step == "lo_part" and s1:
                        lo_part(k, b1)
                    if step == "y_rows" and s2:
                        dve.wait_ge(y_turned.sem, y_turned.at(b2, TILES))
                        yr = ps[:, 0:TILES, 0:QK].rearrange("p t (h s) -> p t h s", h=HEADS)
                        link(chain2, v.reciprocal(row_sum[:], yr[:, :, :, HEAD_DIM]))
                        if later(b2):
                            dve.wait_ge(yt_turned.sem, yt_turned.at(b2 - 1, 2))
                        chained(chain2, b2)
                        for at, first in ((0, 0), (DIM, P // HEAD_DIM)):
                            n = HEADS - first
                            last = v.tensor_tensor(shaped(y_rows[:], [[WIDE, TILES], [HEAD_DIM, n], [1, HEAD_DIM]], at),
                                                   yr[:, :, first:HEADS, 0:HEAD_DIM],
                                                   shaped(row_sum[:], [[HEADS, TILES], [1, n], [0, HEAD_DIM]], first),
                                                   ALU.mult)
                        last.then_inc(y_ready.sem, 1)
                    if step == "y_lo" and s2:
                        keep_low(k, yt, 3, yt_hi, b2, yt_lo)
                    if step == "h1" and s2:
                        for h, n in enumerate((2, 1)):
                            dve.wait_ge(proj_done.sem, proj_done.at(b2, h + 1))
                            dve.wait_ge(res_kept.sem, res_kept.at(b2, 1))
                            last = v.tensor_tensor(h1[:, 2 * h:2 * h + n, :],
                                                   ps[:, 3 + h, 0:n * DIM].rearrange("p (t d) -> p t d", t=n),
                                                   residual[:, 2 * h:2 * h + n, :], ALU.add)
                        last.then_inc(h1_ready.sem, 1)
                    if step == "norm2_stats" and s2 and k:
                        norm_stats(k, chain2, b2, stats2, mean_var2, rstd2)
                    elif step == "norm2_stats" and s2:
                        dve.wait_ge(h1_ready.sem, h1_ready.at(b2, 1))
                        if later(b2):
                            dve.wait_ge(n2_applied.sem, n2_applied.at(b2 - 1, 1))
                        for t in range(TILES):
                            last = v.bn_stats(stats2[:, t, :], h1[:, t, :])
                        link(chain2, last)
                    if step == "norm2_newton" and s2:
                        norm_newton(k, chain2, b2, mean_var2, rstd2, n2_ready)
                    if step == "norm2_lo" and s2:
                        keep_low(k, xt2, 3, xt2_hi, b2, xt2_lo)
                    if step == "router_bias_add" and s2:
                        router_bias_add(b2)
                    if step == "router_pick" and s2:
                        router_pick(k, b2)
                    if step == "gate" and s3:
                        gate(k, b3)
                    if step == "up" and s3:
                        up(k, b3)
                    if step == "sum" and s3:
                        sum_up(k, b3)
                assert not s1 or steps[chain1] == chain1.per_batch, steps[chain1]
                assert not s2 or steps[chain2] == chain2.per_batch, steps[chain2]

            v.memset(h0[:], 0.0).then_inc(s_clear, 1)
            v.memset(v_ones[:], 1.0)
            for j in range(RAW):
                w = slice(j * piece, (j + 1) * piece)
                dve.wait_ge(s_raw[j], 32)
                v.tensor_copy(wa_hi[:, w], raw_a[j]).then_inc(s_split, 1)
                v.tensor_copy(wb[:, w], raw_b[j]).then_inc(s_split, 1)
                dve.wait_ge(s_split, 4 * j + 2)
                v.tensor_tensor(wa_lo[:, w], raw_a[j], f32(wa_hi[:, w]), ALU.subtract).then_inc(s_split, 1)
                v.tensor_tensor(wb[REST:P, w], raw_b[j][REST:P], f32(wb[REST:P, w]), ALU.subtract).then_inc(s_split, 1)
            dve.wait_ge(s_down, 16)
            v.tensor_scalar(w_down_s[:], w_down_s[:], 0.5, None, ALU.mult).then_inc(s_halve, 1)
            dve.wait_ge(s_const, 16 * 9)
            v.tensor_copy(ident_r[:], ident[:]).then_inc(s_halve, 1)
            dve.wait_ge(s_split, 4 * RAW)
            turns(dve, turn)


def kernel(x, txt, L0_tok_W_lin, L0_tok_b_lin, L0_tok_cls_token, L0_attn_qkv_w, L0_attn_c_proj_w,
           L0_ffn_shared_gate, L0_ffn_shared_up, L0_ffn_shared_down, L0_ffn_routed_gate, L0_ffn_routed_up,
           L0_ffn_routed_down, L0_ffn_router_w, L0_ffn_routing_bias):
    import numpy as np
    import concourse.bacc as bacc
    from concourse.bass_utils import run_bass_kernel_spmd

    x, txt = np.asarray(x), np.asarray(txt)
    xp = x.reshape(BATCH, CHANNELS, GRID, PATCH, GRID, PATCH).transpose(0, 1, 3, 5, 2, 4)
    xp = xp.reshape(BATCH, KT, P, PATCHES).transpose(0, 2, 1, 3)
    w_tok = np.asarray(L0_tok_W_lin).T.reshape(KT, P, DIM).transpose(1, 0, 2)
    qkv = np.asarray(L0_attn_qkv_w).transpose(2, 0, 1).reshape(DIM, 3 * DIM)
    proj = np.asarray(L0_attn_c_proj_w).T
    gates = [np.asarray(L0_ffn_shared_gate), *np.asarray(L0_ffn_routed_gate)]
    ups = [np.asarray(L0_ffn_shared_up), *np.asarray(L0_ffn_routed_up)]
    w = np.concatenate([qkv, proj, *[a for pair in zip(gates, ups) for a in pair],
                        np.asarray(L0_ffn_router_w), np.zeros((DIM, R_COLS - EXPERTS), np.float32)], axis=1)
    w_a, w_b = w[:P], np.concatenate([w[P:], w[P:]], axis=0)
    downs = np.concatenate([np.asarray(L0_ffn_shared_down)[None], np.asarray(L0_ffn_routed_down)], axis=0)
    w_down = downs.reshape(UNITS, P, DIM).transpose(1, 0, 2)

    row = np.arange(P)
    pos = np.stack([np.where(row < PATCHES0, row + 1, 0), REAL0 + row, REAL0 + P + row], axis=1).astype(np.float32)
    freqs = (np.float32(1.0 / 1024.0) ** np.linspace(0.0, 1.0, HEAD_DIM // 4, dtype=np.float32)).astype(np.float32)
    theta = pos[:, :, None] * freqs
    cos, sin = np.cos(theta).astype(np.float32), np.sin(theta).astype(np.float32)
    half_cos = np.concatenate([cos, np.ones_like(cos)], axis=2)
    rot_cos = np.concatenate([half_cos, half_cos], axis=2)
    rot_sin = np.concatenate([sin, -sin], axis=2)
    p0 = np.where(np.arange(COLS0) < PATCHES0, np.arange(COLS0) + 1, 0)
    mask0 = (p0[:REAL0, None] <= p0[None, :]).astype(np.float32)
    mask1 = np.triu(np.ones((P, P), np.float32))

    sent = {
        "xp": xp, "txt": txt, "w_tok": w_tok, "bias": np.asarray(L0_tok_b_lin).reshape(1, DIM),
        "cls": np.asarray(L0_tok_cls_token), "w_a": w_a, "w_b": w_b, "w_down": w_down,
        "b_router": np.asarray(L0_ffn_routing_bias).reshape(1, EXPERTS),
        "rot_cos": rot_cos, "rot_sin": rot_sin, "mask0": mask0, "mask1": mask1,
        "identity": np.eye(P, dtype=np.float32),
    }
    nc = bacc.Bacc("TRN2", target_bir_lowering=False, num_devices=1)
    arrays, args = {}, {}
    for name, a in sent.items():
        a = np.ascontiguousarray(a)
        arrays[f"in_{name}"] = a
        args[name] = nc.dram_tensor(f"in_{name}", a.shape, mybir.dt.from_np(a.dtype), kind="ExternalInput").ap()
    for name in ("bias", "b_router"):
        args[name] = args[name][0]
    out = nc.dram_tensor("out_0", (BATCH, TOKENS, DIM), F32, kind="ExternalOutput").ap()
    build(nc, out=out, **args)
    r = run_bass_kernel_spmd(nc, [arrays], core_ids=[0])
    return r.results[0]["out_0"]
```
